# Optimizing a Trainium2 kernel written in Bass

```python
import numpy as np
import jax
import jax.numpy as jnp

def _softmax(x, axis=-1):
    return jax.nn.softmax(x, axis=axis)

def _gelu(x):
    return jax.nn.gelu(x, approximate=True)

def _silu(x):
    return jax.nn.silu(x)

def _sigmoid(x):
    return jax.nn.sigmoid(x)

def _layernorm(x, axis=-1, eps=1e-05):
    m = jnp.mean(x, axis=axis, keepdims=True)
    v = jnp.var(x, axis=axis, keepdims=True)
    return (x - m) / jnp.sqrt(v + eps)

def _scatter_add(tgt, idx, src, axis=0):
    return tgt.at[idx].add(src)

def _segment_sum(src, seg, n):
    return jax.ops.segment_sum(src, seg, n)
kernel_name = 'mk_seq_postln_d2_jaxref_r8_7e7147'

def setup_inputs(seed: int=0):
    np.random.seed(seed)
    _w = jnp.asarray

    def _L0_attn_setup():
        import jax, jax.numpy as jnp
        import numpy as np
        N_HEADS = 16
        key = jax.random.key(seed)
        k1, k2, k3 = jax.random.split(key, 3)
        B, T, C = (4, 256, 128)
        x = jax.random.normal(k1, (B, T, C), dtype=jnp.float32)
        w_qkv = jax.random.normal(k2, (C, 3 * C), dtype=jnp.float32) * (1.0 / np.sqrt(C))
        w_out = jax.random.normal(k3, (C, C), dtype=jnp.float32) * (1.0 / np.sqrt(C))
        return {'x': x, 'w_qkv': w_qkv, 'w_out': w_out}
    _L0_attn_in = _L0_attn_setup()

    def _L0_ffn_setup():
        import jax, jax.numpy as jnp
        import numpy as np
        D_IN, D_HID = (128, 512)

        def _ternary(key, shape):
            return jax.random.randint(key, shape, -1, 2).astype(jnp.float32)

        def _tlin(x, w, s):
            return jnp.einsum('bsi,oi->bso', x, w) * s
        key = jax.random.key(seed)
        ks = jax.random.split(key, 12)
        inv = lambda fan: 1.0 / np.sqrt(fan).astype(np.float32)
        return {'x': jax.random.normal(ks[0], (4, 256, D_IN), dtype=jnp.float32), 'w1_w': _ternary(ks[1], (D_HID, D_IN)), 'w1_s': jax.random.uniform(ks[2], (D_HID,), dtype=jnp.float32) * inv(D_IN), 'w2_w': _ternary(ks[3], (D_HID, D_IN)), 'w2_s': jax.random.uniform(ks[4], (D_HID,), dtype=jnp.float32) * inv(D_IN), 'h1_w': _ternary(ks[5], (D_HID, D_HID)), 'h1_s': jax.random.uniform(ks[6], (D_HID,), dtype=jnp.float32) * inv(D_HID), 'h2_w': _ternary(ks[7], (D_HID, D_HID)), 'h2_s': jax.random.uniform(ks[8], (D_HID,), dtype=jnp.float32) * inv(D_HID), 'w3_w': _ternary(ks[9], (D_IN, D_HID)), 'w3_s': jax.random.uniform(ks[10], (D_IN,), dtype=jnp.float32) * inv(D_HID)}
    _L0_ffn_in = _L0_ffn_setup()

    def _L1_attn_setup():
        import jax, jax.numpy as jnp
        import numpy as np
        B, S, DIM = (2, 1024, 128)
        NH, NKV, HD = (16, 4, 64)
        GROUPS = NH // NKV
        CHUNK = 128
        THETA = 10000.0

        def _slopes(h):
            return jnp.asarray([2.0 ** (-8.0 / h * (i + 1)) for i in range(h)], dtype=jnp.float32)

        def _rope_tables(s, d):
            inv = 1.0 / THETA ** (np.arange(0, d, 2, dtype=np.float64) / d)
            freqs = np.outer(np.arange(s, dtype=np.float64), inv)
            emb = np.concatenate([freqs, freqs], axis=-1)
            return (jnp.asarray(np.cos(emb), jnp.float32), jnp.asarray(np.sin(emb), jnp.float32))

        def _apply_rope(x, cos, sin):
            x1, x2 = jnp.split(x, 2, axis=-1)
            rot = jnp.concatenate([-x2, x1], axis=-1)
            return x * cos + rot * sin

        def _lightning_attn(q, k, v, slopes, chunk):
            b, h, s, d = q.shape
            nc = s // chunk
            t = jnp.arange(chunk, dtype=jnp.float32)
            sl = slopes[:, None, None]
            mask = jnp.where(t[:, None] >= t[None, :], jnp.exp(-sl * (t[:, None] - t[None, :])), 0.0)
            q_dec = jnp.exp(-slopes[:, None] * (t + 1.0))[..., None]
            k_dec = jnp.exp(-slopes[:, None] * (chunk - 1.0 - t))[..., None]
            blk_dec = jnp.exp(-slopes * chunk)[None, :, None, None]

            def to_chunks(x):
                return x.reshape(b, h, nc, chunk, d).transpose(2, 0, 1, 3, 4)
            qc, kc, vc = (to_chunks(q), to_chunks(k), to_chunks(v))

            def step(kv, inp):
                qi, ki, vi = inp
                scores = jnp.einsum('bhtd,bhsd->bhts', qi, ki) * mask
                o = jnp.einsum('bhts,bhsd->bhtd', scores, vi) + jnp.einsum('bhtd,bhde->bhte', qi * q_dec, kv)
                kv = blk_dec * kv + jnp.einsum('bhtd,bhte->bhde', ki * k_dec, vi)
                return (kv, o)
            kv0 = jnp.zeros((b, h, d, d), q.dtype)
            _, outs = jax.lax.scan(step, kv0, (qc, kc, vc))
            return outs.transpose(1, 2, 0, 3, 4).reshape(b, h, s, d)
        key = jax.random.key(seed)
        k0, k1, k2, k3, k4 = jax.random.split(key, 5)
        x = jax.random.normal(k0, (B, S, DIM), jnp.float32)
        Wq = jax.random.normal(k1, (NH * HD, DIM), jnp.float32) * 0.02
        Wk = jax.random.normal(k2, (NKV * HD, DIM), jnp.float32) * 0.02
        Wv = jax.random.normal(k3, (NKV * HD, DIM), jnp.float32) * 0.02
        Wo = jax.random.normal(k4, (DIM, NH * HD), jnp.float32) * 0.02
        return {'x': x, 'Wq': Wq, 'Wk': Wk, 'Wv': Wv, 'Wo': Wo}
    _L1_attn_in = _L1_attn_setup()

    def _L1_ffn_setup():
        import jax, jax.numpy as jnp
        import numpy as np
        B, P, D, D_MLP, E, K = (2, 256, 128, 512, 8, 2)
        key = jax.random.key(seed)
        k_x, k_g, k_in, k_out = jax.random.split(key, 4)
        s_in = 1.0 / np.sqrt(D).astype(np.float32)
        s_out = 1.0 / np.sqrt(D_MLP).astype(np.float32)
        return {'x': jax.random.normal(k_x, (B, P, D), dtype=jnp.float32), 'W_gate': jax.random.normal(k_g, (D, E), dtype=jnp.float32) * s_in, 'W_in': jax.random.normal(k_in, (E, D, D_MLP), dtype=jnp.float32) * s_in, 'b_in': jnp.zeros((E, D_MLP), dtype=jnp.float32), 'W_out': jax.random.normal(k_out, (E, D_MLP, D), dtype=jnp.float32) * s_out, 'b_out': jnp.zeros((E, D), dtype=jnp.float32)}
    _L1_ffn_in = _L1_ffn_setup()
    _d = {'L0_attn_x': _L0_attn_in['x'], 'L0_attn_w_qkv': _L0_attn_in['w_qkv'], 'L0_attn_w_out': _L0_attn_in['w_out'], 'L0_ffn_w1_w': _L0_ffn_in['w1_w'], 'L0_ffn_w1_s': _L0_ffn_in['w1_s'], 'L0_ffn_w2_w': _L0_ffn_in['w2_w'], 'L0_ffn_w2_s': _L0_ffn_in['w2_s'], 'L0_ffn_h1_w': _L0_ffn_in['h1_w'], 'L0_ffn_h1_s': _L0_ffn_in['h1_s'], 'L0_ffn_h2_w': _L0_ffn_in['h2_w'], 'L0_ffn_h2_s': _L0_ffn_in['h2_s'], 'L0_ffn_w3_w': _L0_ffn_in['w3_w'], 'L0_ffn_w3_s': _L0_ffn_in['w3_s'], 'L1_attn_Wq': _L1_attn_in['Wq'], 'L1_attn_Wk': _L1_attn_in['Wk'], 'L1_attn_Wv': _L1_attn_in['Wv'], 'L1_attn_Wo': _L1_attn_in['Wo'], 'L1_ffn_W_gate': _L1_ffn_in['W_gate'], 'L1_ffn_W_in': _L1_ffn_in['W_in'], 'L1_ffn_b_in': _L1_ffn_in['b_in'], 'L1_ffn_W_out': _L1_ffn_in['W_out'], 'L1_ffn_b_out': _L1_ffn_in['b_out']}
    _x0 = _d['L0_attn_x']
    _d['L0_attn_x'] = jax.random.normal(jax.random.fold_in(jax.random.key(seed), 1), (4, 1024, 128), dtype=_x0.dtype)
    del _x0
    return _d

def reference(L0_attn_x, L0_attn_w_qkv, L0_attn_w_out, L0_ffn_w1_w, L0_ffn_w1_s, L0_ffn_w2_w, L0_ffn_w2_s, L0_ffn_h1_w, L0_ffn_h1_s, L0_ffn_h2_w, L0_ffn_h2_s, L0_ffn_w3_w, L0_ffn_w3_s, L1_attn_Wq, L1_attn_Wk, L1_attn_Wv, L1_attn_Wo, L1_ffn_W_gate, L1_ffn_W_in, L1_ffn_b_in, L1_ffn_W_out, L1_ffn_b_out):

    def _L0_attn_ref(x, w_qkv, w_out):
        import jax, jax.numpy as jnp
        import numpy as np
        N_HEADS = 16
        B, T, C = x.shape
        H = N_HEADS
        D = C // H
        qkv = x @ w_qkv
        q, k, v = jnp.split(qkv, 3, axis=-1)
        q = q.reshape(B, T, H, D).transpose(0, 2, 1, 3)
        k = k.reshape(B, T, H, D).transpose(0, 2, 1, 3)
        v = v.reshape(B, T, H, D).transpose(0, 2, 1, 3)
        scale = 1.0 / np.sqrt(D)
        scores = jnp.einsum('bhqd,bhkd->bhqk', q, k) * scale
        causal = jnp.tril(jnp.ones((T, T), dtype=bool))
        scores = jnp.where(causal[None, None, :, :], scores, -jnp.inf)
        weights = jax.nn.softmax(scores, axis=-1)
        out = jnp.einsum('bhqk,bhkd->bhqd', weights, v)
        out = out.transpose(0, 2, 1, 3).reshape(B, T, C)
        return out @ w_out

    def _L0_ffn_ref(x, w1_w, w1_s, w2_w, w2_s, h1_w, h1_s, h2_w, h2_s, w3_w, w3_s):
        import jax, jax.numpy as jnp
        import numpy as np
        D_IN, D_HID = (128, 512)

        def _ternary(key, shape):
            return jax.random.randint(key, shape, -1, 2).astype(jnp.float32)

        def _tlin(x, w, s):
            return jnp.einsum('bsi,oi->bso', x, w) * s
        h = jax.nn.silu(_tlin(x, w1_w, w1_s)) * _tlin(x, w2_w, w2_s)
        h = jax.nn.gelu(_tlin(h, h1_w, h1_s), approximate=False)
        h = jax.nn.gelu(_tlin(h, h2_w, h2_s), approximate=False)
        return _tlin(h, w3_w, w3_s)

    def _L1_attn_ref(x, Wq, Wk, Wv, Wo):
        import jax, jax.numpy as jnp
        import numpy as np
        B, S, DIM = (2, 1024, 128)
        NH, NKV, HD = (16, 4, 64)
        GROUPS = NH // NKV
        CHUNK = 128
        THETA = 10000.0

        def _slopes(h):
            return jnp.asarray([2.0 ** (-8.0 / h * (i + 1)) for i in range(h)], dtype=jnp.float32)

        def _rope_tables(s, d):
            inv = 1.0 / THETA ** (np.arange(0, d, 2, dtype=np.float64) / d)
            freqs = np.outer(np.arange(s, dtype=np.float64), inv)
            emb = np.concatenate([freqs, freqs], axis=-1)
            return (jnp.asarray(np.cos(emb), jnp.float32), jnp.asarray(np.sin(emb), jnp.float32))

        def _apply_rope(x, cos, sin):
            x1, x2 = jnp.split(x, 2, axis=-1)
            rot = jnp.concatenate([-x2, x1], axis=-1)
            return x * cos + rot * sin

        def _lightning_attn(q, k, v, slopes, chunk):
            b, h, s, d = q.shape
            nc = s // chunk
            t = jnp.arange(chunk, dtype=jnp.float32)
            sl = slopes[:, None, None]
            mask = jnp.where(t[:, None] >= t[None, :], jnp.exp(-sl * (t[:, None] - t[None, :])), 0.0)
            q_dec = jnp.exp(-slopes[:, None] * (t + 1.0))[..., None]
            k_dec = jnp.exp(-slopes[:, None] * (chunk - 1.0 - t))[..., None]
            blk_dec = jnp.exp(-slopes * chunk)[None, :, None, None]

            def to_chunks(x):
                return x.reshape(b, h, nc, chunk, d).transpose(2, 0, 1, 3, 4)
            qc, kc, vc = (to_chunks(q), to_chunks(k), to_chunks(v))

            def step(kv, inp):
                qi, ki, vi = inp
                scores = jnp.einsum('bhtd,bhsd->bhts', qi, ki) * mask
                o = jnp.einsum('bhts,bhsd->bhtd', scores, vi) + jnp.einsum('bhtd,bhde->bhte', qi * q_dec, kv)
                kv = blk_dec * kv + jnp.einsum('bhtd,bhte->bhde', ki * k_dec, vi)
                return (kv, o)
            kv0 = jnp.zeros((b, h, d, d), q.dtype)
            _, outs = jax.lax.scan(step, kv0, (qc, kc, vc))
            return outs.transpose(1, 2, 0, 3, 4).reshape(b, h, s, d)
        b, s, _ = x.shape
        q = (x @ Wq.T).reshape(b, s, NH, HD).transpose(0, 2, 1, 3)
        k = (x @ Wk.T).reshape(b, s, NKV, HD).transpose(0, 2, 1, 3)
        v = (x @ Wv.T).reshape(b, s, NKV, HD).transpose(0, 2, 1, 3)
        cos, sin = _rope_tables(s, HD)
        q = _apply_rope(q, cos, sin)
        k = _apply_rope(k, cos, sin)
        k = jnp.repeat(k, GROUPS, axis=1)
        v = jnp.repeat(v, GROUPS, axis=1)
        out = _lightning_attn(q, k, v, _slopes(NH), CHUNK)
        out = out.transpose(0, 2, 1, 3).reshape(b, s, NH * HD)
        return out @ Wo.T

    def _L1_ffn_ref(x, W_gate, W_in, b_in, W_out, b_out):
        import jax, jax.numpy as jnp
        import numpy as np
        B, P, D, D_MLP, E, K = (2, 256, 128, 512, 8, 2)
        gate_logits = jnp.einsum('bpd,de->bpe', x, W_gate)
        top_w, top_idx = jax.lax.top_k(gate_logits, K)
        top_w = jax.nn.softmax(top_w, axis=-1)
        combine = jnp.einsum('bpke,bpk->bpe', jax.nn.one_hot(top_idx, E, dtype=x.dtype), top_w)
        out = jnp.zeros_like(x)
        for e in range(E):
            h = jax.nn.gelu(jnp.einsum('bpd,dm->bpm', x, W_in[e]) + b_in[e], approximate=False)
            y = jnp.einsum('bpm,md->bpd', h, W_out[e]) + b_out[e]
            out = out + combine[..., e, None] * y
        return out
    x = L0_attn_x
    x = _layernorm(x + _L0_attn_ref(x, L0_attn_w_qkv, L0_attn_w_out), axis=-1)
    x = _layernorm(x + _L0_ffn_ref(x, L0_ffn_w1_w, L0_ffn_w1_s, L0_ffn_w2_w, L0_ffn_w2_s, L0_ffn_h1_w, L0_ffn_h1_s, L0_ffn_h2_w, L0_ffn_h2_s, L0_ffn_w3_w, L0_ffn_w3_s), axis=-1)
    x = _layernorm(x + _L1_attn_ref(x, L1_attn_Wq, L1_attn_Wk, L1_attn_Wv, L1_attn_Wo), axis=-1)
    x = _layernorm(x + _L1_ffn_ref(x, L1_ffn_W_gate, L1_ffn_W_in, L1_ffn_b_in, L1_ffn_W_out, L1_ffn_b_out), axis=-1)
    return x

_drawn_inputs = setup_inputs


def setup_inputs(seed=0):
    import zlib

    import numpy as np

    out = dict(_drawn_inputs(seed))
    spreads = {'L1_ffn_b_in': (0.0, 0.1), 'L1_ffn_b_out': (0.0, 0.1)}
    factors = {'L0_ffn_w1_w': 3.378,
     'L0_ffn_w1_s': 5.553,
     'L0_ffn_w2_w': 3.269,
     'L0_ffn_w2_s': 5.12,
     'L0_ffn_h1_w': 3.311,
     'L0_ffn_h1_s': 6.304,
     'L0_ffn_h2_w': 3.126,
     'L0_ffn_h2_s': 4.635,
     'L0_ffn_w3_w': 3.45,
     'L0_ffn_w3_s': 5.805}
    for name, (base, spread) in spreads.items():
        noise = np.random.default_rng([zlib.crc32(name.encode()), seed]).standard_normal(out[name].shape)
        drawn = base * np.exp(spread * noise) if base else spread * noise
        out[name] = jnp.asarray(drawn.astype(out[name].dtype))
    for name, factor in factors.items():
        out[name] = (out[name] * factor).astype(out[name].dtype)
    return out
```

```python
from contextlib import ExitStack

import numpy as np

import concourse.bass as bass
from concourse import mybir

F32 = mybir.dt.float32
BF16 = mybir.dt.bfloat16
U32 = mybir.dt.uint32
ALU = mybir.AluOpType
ACT = mybir.ActivationFunctionType
AX = mybir.AxisListType

P = 128
B, T, C = 4, 1024, 128
NT = B * T
EPS = 1e-5

H0, D0 = 16, 8
HQ = 4
NU = B * (H0 // HQ)
KT = T // P
QC = T // 512
PARTS = 3
SROWS = PARTS * PARTS * D0
MROW = 96
SCALE0 = float(D0) ** -0.5
NEG = -1.0e30
NBANK = 3
NSLOT = 12


def exp_plan():
    groups = []
    for qc in range(QC):
        q0 = 512 * qc
        for kt in range(4 * qc + 1):
            groups.append((qc, [[(h, kt, q0, 512, 0)] for h in range(HQ)]))
        a = 4 * qc
        groups.append((qc, [[(h, a + 1, q0 + 128, 384, 0), (h, a + 3, q0 + 384, 128, 384)] for h in range(HQ)]))
        groups.append((qc, [[(h, a + 2, q0 + 256, 256, 256 * (h % 2)) for h in (g, g + 1)] for g in (0, 2)]))
    return groups


def max_plan():
    items = []
    for qt in range(KT):
        for k0 in range(0, P * (qt + 1), 512):
            n = min(512, P * (qt + 1) - k0)
            whole = n == P or (n == 256 and k0)
            items += [(qt, hs, k0, n) for hs in ([range(4)] if whole else [range(2), range(2, 4)])]
    return items


GROUPS = exp_plan()
NG = len(GROUPS)
STEPS = [s for _, g in GROUPS for s in g]
NS = len(STEPS)
DIAGONAL = [g for g, (_, st) in enumerate(GROUPS) if any(x[2] == x[1] * P for y in st for x in y)]
GROUP_OF = [g for g, (_, steps) in enumerate(GROUPS) for _ in steps]
HALF_GROUP = 1 + max(g for g, (_, st) in enumerate(GROUPS) if any(min(x[1] * P, x[2]) < 512 for y in st for x in y))
FIRST_STEP = [GROUP_OF.index(g) for g in range(NG)]
ITEMS = max_plan()
NI = len(ITEMS) + 1
HALF_ITEM = min(k for k, (qt, _, _, _) in enumerate(ITEMS) if qt >= 4)
PER_SLOT = 3
assert NS % NBANK == 0 and NS % NSLOT == 0 and NI % 2 == 0
CHAIN_SLOT = -(-len(ITEMS) // PER_SLOT)
assert CHAIN_SLOT + 1 < NG


H1, KV1, D1 = 16, 4, 64
LATE = ["wo0", "w1", "w2", "h1", "h2", "w3", "s1", "s2", "sh1", "sh2", "s3", "wq", "wqr", "wk", "wkr", "wv", "wo1",
        "mask1", "qdec", "kdec", "bdec", "wgate", "b_in", "b_dn", "iota"]
ARENA = 38400


def program(nc, a, out):
    with ExitStack() as ctx:
        def sb(name, shape, dt=F32):
            return ctx.enter_context(nc.sbuf_tensor(name, shape, dt))

        def sem(name):
            return ctx.enter_context(nc.semaphore(name))

        banks = ctx.enter_context(nc.psum_tensor("banks", [P, 8, 512], F32))
        q_parts = nc.dram_tensor("q_parts", [NU, HQ, PARTS * D0, T], BF16, kind="Internal").ap()
        k_parts = nc.dram_tensor("k_parts", [NU, HQ, PARTS, D0, T], BF16, kind="Internal").ap()
        att_t = nc.dram_tensor("att_t", [NU, HQ, D0, T], F32, kind="Internal").ap()

        ident = sb("ident", [P, P])
        identb = sb("identb", [P, P], BF16)
        mask_qk = sb("mask_qk", [P, P], BF16)
        mask_kq = sb("mask_kq", [P, P], BF16)
        wqkv = sb("wqkv", [P, 3 * C])
        late = {n: sb(n, list(a[n].shape)) for n in LATE}

        arena = sb("arena", [P, ARENA])

        def carve():
            at = [0]

            def view(shape, dt=F32):
                n = int(np.prod(shape[1:]))
                words = n if dt == F32 else n // 2
                v = arena[:, at[0]:at[0] + words]
                at[0] += words
                assert at[0] <= ARENA, at
                if dt != F32:
                    v = v.bitcast(dt)
                if len(shape) > 2:
                    names = " ".join("abcd"[:len(shape) - 1])
                    v = v.rearrange(f"p ({names}) -> p {names}", **dict(zip("abcd", shape[1:])))
                return v
            return view

        view = carve()
        vnat = view([P, NU, KT, HQ * D0])
        xT = view([P, 2, 512])
        qk3 = [[view([P, PARTS, 512], BF16) for w in range(2)] for p in range(2)]
        rest = view([P, 2, 512])
        sq = [view([P, HQ, T], BF16) for p in range(2)]
        sk = [view([P, HQ, T], BF16) for p in range(2)]
        va = [view([P, KT, HQ, 32]) for p in range(2)]
        pe_ = view([P, NSLOT, 512])
        mx = view([P, 2, KT, HQ])
        mm = view([P, KT, HQ])
        mr = view([P, KT, HQ])
        m3 = view([P, KT, HQ, PARTS], BF16)
        mrows = view([P, T], BF16)
        tq = view([P, 16, 32])
        rl = view([P, 16, 1])
        ta = view([P, QC, 512])

        s_cst = sem("s_cst")
        s_w = sem("s_w")
        s_late = sem("s_late")
        s_init = sem("s_init")
        s_xT = [sem(f"s_xT{p}") for p in range(2)]
        s_proj = sem("s_proj")
        s_q1 = sem("s_q1")
        s_r1 = sem("s_r1")
        s_q2 = sem("s_q2")
        s_q3 = sem("s_q3")
        s_v = sem("s_v")
        s_sc = [sem(f"s_sc{p}") for p in range(2)]
        s_st = [[sem(f"s_st{p}{half}") for half in range(2)] for p in range(2)]
        s_va = sem("s_va")
        s_qk = sem("s_qk")
        s_exp = sem("s_exp")
        s_tri = sem("s_tri")
        s_hold = sem("s_hold")
        s_pv = sem("s_pv")
        s_it = sem("s_it")
        s_itc = sem("s_itc")
        s_m = sem("s_m")
        s_m3 = sem("s_m3")
        s_mrow = sem("s_mrow")
        s_t1 = sem("s_t1")
        s_n = sem("s_n")
        s_ta = sem("s_ta")
        s_att = [sem(f"s_att{q}") for q in range(QC)]

        block = ctx.enter_context(nc.Block())
        score = [banks[:, i, :] for i in range(NBANK)]
        pv_bank = banks[:, NBANK, :]
        pair = [banks[:, 4 + 2 * i:6 + 2 * i, :] for i in range(2)]
        q_dst = q_parts.rearrange("(b j) h (a d) t -> b a (j h) d t", b=B, a=PARTS)
        k_dst = k_parts.rearrange("(b j) h a d t -> b a (j h) d t", b=B)

        def units(eng, unit):
            for u in range(2):
                unit(u, u % 2, u == 0, False, 0)
            with_loop(eng, 1, NU // 2 - 1, lambda i: [unit(2 * i + p, p, False, False, i) for p in range(2)])
            for u in range(NU - 2, NU):
                unit(u, u % 2, False, u == NU - 1, u // 2)

        def with_loop(eng, lo, hi, body):
            with eng.Fori(lo, hi) as i:
                body(i)

        view = carve()
        q_all = view([P, 8, 512])
        hid = [q_all[:, 0:4, :], q_all[:, 4:8, :]]
        q_dec = view([P, 4, 4, P])
        k_all = view([P, 2, 512])
        k_one = [view([P, 2, 512]) for _ in range(2)]
        rot_a = view([P, 2, 512])
        rot_b = view([P, 2, 512])
        v_nat = view([P, B, KV1, D1])
        k_nat = view([P, 2, B, P])
        v_dec = view([P, 2, 2, 4, D1])
        sm = view([P, 4, 512])
        o_t = view([P, 4, 4, P])
        state = view([P, B, 2, 4, P])
        cos_c, sin_c = view([P, P]), view([P, P])
        att_c = view([P, B, P])
        x_in = view([P, B, P])
        x1, x1T, x2, x2T, x3, x3T = (view([P, B, P]) for _ in range(6))
        res = view([P, B, P])
        acc = view([P, B, P])
        gated = view([P, 2, 512])
        h_exp = view([P, 8, 512])
        w_in = view([P, 4, 512])
        w_dn = view([P, 4, 4, C])
        stats = view([P, B, 8])
        mv = view([P, B, 2])
        var = view([P, B])
        rstd = view([P, B])
        minus_half = view([P, B])
        spare = view([P, 2])
        logit = view([P, B, 8])
        top8 = view([P, B, 8])
        idxf = view([P, B, 8])
        expd = view([P, B])
        wgt = view([P, 2, B])
        pick = view([P, 2, B, 8])
        comb = view([P, B, 8])
        combT = view([P, 512])
        idx8 = view([P, B, 8]).bitcast(U32)

        NITER = T // P + 1
        x_v = a["x"].rearrange("b (c p) k -> c p b k", p=P)
        out_v = out.rearrange("b (c p) k -> c p b k", p=P)
        att_v = att_t.rearrange("(b j) h d t -> (j h d) b t", b=B)
        lines = ["pe", "act", "dve", "pool", "attc", "xin", "rope", "we0", "we1", "we2", "we3", "out"]
        s_line = {n: sem(f"s_{n}") for n in lines}
        s_off = sem("s_off")

        class Tape:

            def __init__(self, eng, me, it, live, before):
                self.eng, self.me, self.it, self.live, self.before = eng, me, it, live, before
                self.count = {n: 0 for n in lines}
                self.where = {}
                self.seen = {}
                self.null = 0
                self.held = []
                self.part = None

            def wait(self, need):
                name, ago = (need, 0) if isinstance(need, str) else need
                if ago:
                    if self.before is None:
                        return
                    line, k = self.before.where[name]
                    k -= self.before.count[line]
                else:
                    line, k = self.where[name]
                if self.seen.get(line, -10 ** 6) >= k:
                    return
                self.seen[line] = k
                unit = 1 if line in ("pe", "act", "dve", "pool") else 16
                per = self.before.count[line] if self.before else 0
                value = (self.it * per + k) * unit
                if isinstance(value, int) and value <= 0:
                    return
                self.eng.wait_ge(s_line[line], value)

            def flush(self):
                if self.null:
                    per = self.before.count[self.me]
                    done = self.it * per + self.count[self.me] - self.null
                    if done > 0:
                        self.eng.wait_ge(s_line[self.me], done)
                    self.eng.sem_inc(s_line[self.me], self.null)
                    self.null = 0

            def do(self, who, name, needs, fn, line=None, apart=False):
                line = line or who
                unit = 1 if line == who else 16
                if self.me == who and self.eng is not None:
                    if self.part in self.live:
                        self.flush()
                        for n in needs:
                            self.wait(n)
                        if apart:
                            nc.vector.memset(spare, 0.0)
                        fn().then_inc(s_line[line], unit)
                    elif line == who:
                        self.count[line] += 1
                        self.null += 1
                        self.where[name] = (line, self.count[line])
                        return
                    else:
                        self.eng.sem_inc(s_line[line], 16)
                self.count[line] += 1
                self.where[name] = (line, self.count[line])

            def bank(self):
                k = len(self.held)
                self.held.append(None)
                if k >= 8:
                    return k, banks[:, k % 8, :], [self.held[k - 8]]
                if self.before is None:
                    return k, banks[:, k % 8, :], []
                return k, banks[:, k % 8, :], [(self.before.held[len(self.before.held) - 8 + k], 1)]

            def free(self, k, name):
                self.held[k] = name

            def pad_banks(self):
                while len(self.held) % 8:
                    self.held.append(self.held[len(self.held) - 8])

        NE = 8

        def mms(pairs):
            for n, (dst, l, r) in enumerate(pairs):
                ins = nc.tensor.matmul(dst, l, r, start=(n == 0), stop=(n == len(pairs) - 1), skip_group_check=True)
            return ins

        def last(gen):
            for ins in gen:
                pass
            return ins

        def layernorm(tp, tag, need, src, dst, dst_free):
            tp.do("dve", f"stats{tag}", [need], lambda: last(
                nc.vector.bn_stats(stats[:, t, 0:6], src[:, t, :]) for t in range(B)))
            tp.do("dve", f"aggr{tag}", [f"stats{tag}"], lambda: last(
                nc.vector.bn_aggr(mv[:, t, :], stats[:, t, 0:6]) for t in range(B)), apart=True)
            tp.do("dve", f"var{tag}", [f"aggr{tag}"], lambda: nc.vector.tensor_scalar(
                var[:, :], mv[:, :, 1], EPS, None, ALU.add))
            tp.do("pool", f"rstd{tag}", [f"var{tag}"], lambda: nc.gpsimd.tensor_tensor(
                rstd[:, :], var[:, :], minus_half[:, :], ALU.pow))
            tp.do("dve", f"norm{tag}", [f"rstd{tag}"] + dst_free, lambda: last(
                nc.vector.tensor_scalar(dst[:, t, :], src[:, t, :], mv[:, t, 0:1], rstd[:, t:t + 1],
                                        ALU.subtract, ALU.mult) for t in range(B)))

        def turned(tp, tag, src, dst, dst_free):
            k, bk, fr = tp.bank()
            tp.do("pe", f"turn{tag}", [f"norm{tag}"] + fr, lambda: last(
                nc.tensor.transpose(bk[:, t * P:(t + 1) * P], src[:, t, :], ident[:, :]) for t in range(B)))
            tp.do("act", f"turned{tag}", [f"turn{tag}"] + dst_free, lambda: nc.scalar.copy(
                dst.rearrange("p b t -> p (b t)"), bk))
            tp.free(k, f"turned{tag}")

        def body(tp):
            it = tp.it
            c = it - 1

            tp.part = "front"
            tp.do("sp", "att_in", [("outproj", 1)], lambda: nc.sync.dma_start(
                att_c, att_v[:, :, bass.ds(it * P, P)]), line="attc")
            tp.do("sp", "x_in", [("res1", 1)], lambda: nc.sync.dma_start(
                x_in, x_v[bass.ds(it, 1)].rearrange("c p b k -> p (c b) k")), line="xin")
            k, bk, fr = tp.bank()
            tp.do("pe", "outproj", ["att_in"] + fr, lambda: last(
                nc.tensor.matmul(bk[:, t * P:(t + 1) * P], att_c[:, t, :], late["wo0"][:, :], start=True, stop=True)
                for t in range(B)))
            tp.do("dve", "res1", ["outproj", "x_in", ("norm4", 1)], lambda: nc.vector.tensor_tensor(
                res, bk.rearrange("p (b c) -> p b c", b=B), x_in, ALU.add))
            tp.free(k, "res1")
            layernorm(tp, 1, "res1", res, x1, [("turn1", 1), ("res2", 1)])

            tp.part = "rear"
            tp.do("sp", "rope", [("turn_b9", 1)], lambda: nc.sync.dma_start(
                cos_c, a["cos"][:, bass.ds(c * P, P)]), line="rope")
            tp.do("sp", "rope2", [], lambda: nc.sync.dma_start(
                sin_c, a["sin"][:, bass.ds(c * P, P)]), line="rope")
            for e in range(4):
                load_expert(tp, e)
            xt = x2T.rearrange("p b t -> p (b t)")
            for n in range(10):
                wa = late["wq"][:, n, :] if n < 8 else late["wk"][:, n - 8, :]
                wb = late["wqr"][:, n, :] if n < 8 else late["wkr"][:, n - 8, :]
                slot = n % 2
                used = f"rot{n - 2}" if n >= 2 else ("rot" + str(8 + n), 1)
                for w, tab, buf, nm in ((wa, cos_c, rot_a, "a"), (wb, sin_c, rot_b, "b")):
                    k, bk, fr = tp.bank()
                    tp.do("pe", f"proj{nm}{n}", [("turned2", 1)] + fr, lambda: nc.tensor.matmul(
                        bk, w, xt, start=True, stop=True))
                    tp.do("dve", f"turn_{nm}{n}", ["rope2", f"proj{nm}{n}", used], lambda: nc.vector.tensor_tensor(
                        buf[:, slot, :].rearrange("p (b t) -> p b t", b=B), bk.rearrange("p (b t) -> p b t", b=B),
                        tab.rearrange("p (o t) -> p o t", o=1).to_broadcast([P, B, P]), ALU.mult))
                    tp.free(k, f"turn_{nm}{n}")
                dst = q_all[:, n, :] if n < 8 else k_all[:, n - 8, :]
                tp.do("pool", f"rot{n}", [f"turn_b{n}", ("down0", 1) if n < 8 else ("kt_last", 1)],
                      lambda: nc.gpsimd.tensor_tensor(dst, rot_a[:, slot, :], rot_b[:, slot, :], ALU.add))
            for kp in range(2):
                tp.do("act", f"k_one{kp}", [f"rot{8 + kp}", ("scores_last", 1)], lambda: last(nc.scalar.copy(
                    k_one[i][64 * i:64 * i + 64, kp, :], k_all[64 * i:64 * i + 64, kp, :]) for i in range(2)))
            for g in range(2):
                k, bk, fr = tp.bank()
                tp.do("pe", f"v{g}", fr, lambda: last(nc.tensor.matmul(
                    bk[:, 256 * i:256 * i + 256], x2T[:, 2 * g + i, :], late["wv"][:, :], start=True, stop=True)
                    for i in range(2)))
                tp.do("act", f"vn{g}", [f"v{g}", ("vdec_last", 1), ("attn_last", 1)], lambda: nc.scalar.copy(
                    v_nat[:, 2 * g:2 * g + 2, :, :].rearrange("p b g d -> p (b g d)"), bk))
                tp.free(k, f"vn{g}")
            for kp in range(2):
                k, bk, fr = tp.bank()
                tp.do("pe", f"kt{kp}", [f"rot{8 + kp}"] + fr, lambda: last(nc.tensor.transpose(
                    bk[:, t * P:(t + 1) * P], k_all[:, kp, t * P:(t + 1) * P], ident[:, :]) for t in range(B)))
                tp.do("act", f"kn{kp}", [f"kt{kp}", ("grow_last", 1)], lambda: nc.scalar.copy(
                    k_nat[:, kp, :, :].rearrange("p b d -> p (b d)"), bk))
                tp.free(k, f"kn{kp}")

            def scores1(n):
                b, kp = divmod(n, 2)
                tp.do("pool", f"qdec{n}", [f"rot{4 * kp + 3}", f"attn{n - 4}" if n >= 4 else (f"attn{n + 4}", 1)],
                      lambda: nc.gpsimd.tensor_tensor(
                    q_dec[:, n % 4, :, :], q_all[:, 4 * kp:4 * kp + 4, b * P:(b + 1) * P],
                    late["qdec"][:, 4 * kp:4 * kp + 4, :], ALU.mult))
                tp.do("pool", f"vdec{n}", ["vn1", f"grow{n - 2}" if n >= 2 else (f"grow{n + 6}", 1)],
                      lambda: nc.gpsimd.tensor_tensor(
                    v_dec[:, n % 2, :, :, :].rearrange("p g i d -> p (g i) d"),
                    v_nat[:, b, 2 * kp:2 * kp + 2, :].rearrange("p (g o) d -> p g o d", o=1)
                    .to_broadcast([P, 2, 4, D1]).rearrange("p g i d -> p g i d"),
                    late["kdec"][:, 8 * kp:8 * kp + 8].rearrange("p (g i o) -> p g i o", g=2, o=1)
                    .to_broadcast([P, 2, 4, D1]), ALU.mult))
                for i in range(2):
                    k, bk, fr = tp.bank()
                    s = (2 * n + i) % 4
                    prev = f"attn{n - 2}" if n >= 2 else (f"attn{n + 6}", 1)
                    tp.do("pe", f"scores{n}{i}", [f"k_one{kp}", f"rot{4 * kp + 3}"] + fr, lambda: nc.tensor.matmul(
                        bk, k_one[i][:, kp, b * P:(b + 1) * P], q_all[:, 4 * kp:4 * kp + 4, b * P:(b + 1) * P],
                        start=True, stop=True))
                    tp.do("dve", f"masked{n}{i}", [f"scores{n}{i}", prev], lambda: nc.vector.tensor_tensor(
                        sm[:, s, :], bk, late["mask1"][:, 512 * (2 * kp + i):512 * (2 * kp + i) + 512], ALU.mult))
                    tp.free(k, f"masked{n}{i}")

            def attend(n):
                b, kp = divmod(n, 2)
                k, bk, fr = tp.bank()

                def products():
                    for i in range(2):
                        nc.tensor.matmul(bk[64 * i:64 * i + 64, :], v_nat[:, b, 2 * kp + i, :], sm[:, (2 * n + i) % 4, :],
                                         start=True, stop=False, skip_group_check=True)
                    for i in range(4):
                        ins = nc.tensor.matmul(bk[:, i * P:(i + 1) * P], state[:, b, kp, i, :], q_dec[:, n % 4, i, :],
                                               start=False, stop=True, skip_group_check=True)
                    return ins
                tp.do("pe", f"attn{n}", [f"masked{n}1", f"qdec{n}", (f"state{n}", 1)] + fr, products)
                used = (f"y{n // 2 + 2}", 1) if n < 4 else f"y{n // 2 - 2}"
                tp.do("act", f"o{n}", [f"attn{n}", used], lambda: nc.scalar.copy(
                    o_t[:, n % 4, :, :].rearrange("p i t -> p (i t)"), bk))
                tp.free(k, f"o{n}")
                k, bk, fr = tp.bank()
                tp.do("pe", f"grow{n}", [f"kn{kp}", f"vdec{n}"] + fr, lambda: last(nc.tensor.matmul(
                    bk[64 * i:64 * i + 64, 0:256], k_nat[:, kp, b, 64 * i:64 * i + 64],
                    v_dec[:, n % 2, i, :, :].rearrange("p h d -> p (h d)"), start=True, stop=True,
                    skip_group_check=True) for i in range(2)))

                tp.do("pool", f"decay{n}", [f"attn{n}", (f"state{n}", 1)], lambda: nc.gpsimd.tensor_tensor(
                    state[:, b, kp, :, :], state[:, b, kp, :, :],
                    late["bdec"][:, 4 * kp:4 * kp + 4].rearrange("p (i o) -> p i o", o=1).to_broadcast([P, 4, P]),
                    ALU.mult))

                def grow():
                    for i in range(2):
                        h = slice(64 * i, 64 * i + 64)
                        st = state[h, b, kp, :, 64 * i:64 * i + 64]
                        ins = nc.vector.tensor_tensor(st, bk[h, 0:256].rearrange("p (i d) -> p i d", i=4), st, ALU.add)
                    return ins
                tp.do("dve", f"state{n}", [f"grow{n}", f"decay{n}"], grow)
                tp.free(k, f"state{n}")

            def project1(b):
                k, bk, fr = tp.bank()
                tp.do("pe", f"y{b}", [f"o{2 * b + 1}"] + fr, lambda: mms(
                    [(bk[:, 0:P], o_t[:, (2 * b + kp) % 4, i, :], late["wo1"][:, 4 * kp + i, :])
                     for kp in range(2) for i in range(4)]))
                tp.do("dve", f"res3_{b}", [f"y{b}", "norm1"], lambda: nc.vector.tensor_tensor(
                    res[:, b, :], bk[:, 0:P], x2[:, b, :], ALU.add))
                tp.free(k, f"res3_{b}")

            scores1(0)
            for n in range(8):
                if n < 7:
                    scores1(n + 1)
                attend(n)
                if n in (2, 4, 6):
                    project1(n // 2 - 1)
            for new, old in (("scores_last", "scores71"), ("vdec_last", "vdec7"), ("attn_last", "attn7"),
                             ("grow_last", "grow7"), ("kt_last", "kt1")):
                tp.where[new] = tp.where[old]

            tp.part = "front"
            turned(tp, 1, x1, x1T, [("up_b3", 1)])
            tp.part = "rear"
            project1(3)
            layernorm(tp, 3, "res3_3", res, x3, ["turn1", ("stored", 1)])
            tp.part = "front"
            xt1 = x1T.rearrange("p b t -> p (b t)")
            for m in range(4):
                k, bk, fr = tp.bank()
                tp.do("pe", f"up_a{m}", ["turned1"] + fr, lambda: nc.tensor.matmul(
                    bk, late["w1"][:, m * P:(m + 1) * P], xt1, start=True, stop=True))
                tp.do("act", f"silu{m}", [f"up_a{m}", f"mul{m - 2}" if m >= 2 else (f"mul{m + 2}", 1)],
                      lambda: nc.scalar.activation(gated[:, m % 2, :], bk, ACT.Silu, scale=late["s1"][:, m:m + 1]))
                tp.free(k, f"silu{m}")
                k, bk, fr = tp.bank()
                tp.do("pe", f"up_b{m}", fr, lambda: nc.tensor.matmul(
                    bk, late["w2"][:, m * P:(m + 1) * P], xt1, start=True, stop=True))
                tp.do("dve", f"mul{m}", [f"up_b{m}", f"silu{m}", "scores_last", "qdec7"],
                      lambda: nc.vector.scalar_tensor_tensor(
                    out=hid[0][:, m, :], in0=bk, scalar=late["s2"][:, m:m + 1], in1=gated[:, m % 2, :],
                    op0=ALU.mult, op1=ALU.mult))
                tp.free(k, f"mul{m}")
            tp.part = "rear"
            turned(tp, 3, x3, x3T, [("up_e7", 1)])

            def hidden(i, src, dst, need):
                for m in range(4):
                    k, bk, fr = tp.bank()
                    tp.do("pe", f"hid{i}_{m}", [need] + fr, lambda: mms(
                        [(bk, late[f"h{i}"][:, kk, m * P:(m + 1) * P], src[:, kk, :]) for kk in range(4)]))
                    tp.do("act", f"gelu{i}_{m}", [f"hid{i}_{m}"], lambda: nc.scalar.activation(
                        dst[:, m, :], bk, ACT.Gelu, scale=late[f"sh{i}"][:, m:m + 1]))
                    tp.free(k, f"gelu{i}_{m}")
            tp.part = "front"
            hidden(1, hid[0], hid[1], "mul3")

            tp.part = "rear"
            k, bk, fr = tp.bank()
            tp.do("pe", "gate", ["turned3"] + fr, lambda: last(nc.tensor.matmul(
                bk[:, 8 * t:8 * t + 8], x3T[:, t, :], late["wgate"][:, :], start=True, stop=True) for t in range(B)))
            tp.do("dve", "logit", ["gate"], lambda: nc.vector.tensor_copy(
                logit.rearrange("p b e -> p (b e)"), bk[:, 0:32]))
            tp.free(k, "logit")
            tp.do("dve", "top", ["logit"], lambda: last(
                nc.vector.max(top8[:, t, :], logit[:, t, :]) for t in range(B)), apart=True)
            tp.do("dve", "index", ["top"], lambda: last(
                nc.vector.max_index(idx8[:, t, :], top8[:, t, :], logit[:, t, :]) for t in range(B)), apart=True)
            tp.do("dve", "gap", ["top"], lambda: nc.vector.tensor_tensor(
                expd, top8[:, :, 1], top8[:, :, 0], ALU.subtract))
            tp.do("act", "exp", ["gap"], lambda: nc.scalar.activation(wgt[:, 1, :], expd, ACT.Exp))
            tp.do("dve", "indexf", ["index"], lambda: nc.vector.tensor_copy(idxf, idx8))
            tp.do("dve", "onehot", ["indexf"], lambda: last(nc.vector.tensor_tensor(
                pick[:, i, :, :], late["iota"][:, :].rearrange("p (o e) -> p o e", o=1).to_broadcast([P, B, 8]),
                idxf[:, :, i:i + 1].to_broadcast([P, B, 8]), ALU.is_equal) for i in range(2)))
            tp.do("dve", "denom", ["exp"], lambda: nc.vector.tensor_scalar(
                wgt[:, 0, :], wgt[:, 1, :], 1.0, None, ALU.add))
            tp.do("dve", "first", ["denom"], lambda: nc.vector.reciprocal(wgt[:, 0, :], wgt[:, 0, :]))
            tp.do("dve", "second", ["first"], lambda: nc.vector.tensor_tensor(
                wgt[:, 1, :], wgt[:, 1, :], wgt[:, 0, :], ALU.mult))
            tp.do("dve", "picked", ["second", "onehot"], lambda: last(nc.vector.tensor_tensor(
                pick[:, i, :, :], pick[:, i, :, :],
                wgt[:, i, :].rearrange("p (b o) -> p b o", o=1).to_broadcast([P, B, 8]), ALU.mult) for i in range(2)))
            tp.do("dve", "comb", ["picked", ("combine7", 1)], lambda: nc.vector.tensor_tensor(
                comb, pick[:, 0, :, :], pick[:, 1, :, :], ALU.add))

            tp.part = "front"
            hidden(2, hid[1], hid[0], "gelu1_3")
            k, bk, fr = tp.bank()
            tp.do("pe", "down0", ["gelu2_3"] + fr, lambda: last(mms(
                [(bk[:, t * P:(t + 1) * P], hid[0][:, kk, t * P:(t + 1) * P], late["w3"][:, kk, :])
                 for kk in range(4)]) for t in range(B)))
            tp.do("dve", "scale2", ["down0", "norm3"], lambda: nc.vector.tensor_tensor(
                res, bk.rearrange("p (b c) -> p b c", b=B),
                late["s3"][:, :].rearrange("p (o c) -> p o c", o=1).to_broadcast([P, B, C]), ALU.mult))
            tp.free(k, "scale2")
            tp.do("dve", "res2", ["scale2"], lambda: nc.vector.tensor_tensor(res, res, x1, ALU.add))
            layernorm(tp, 2, "res2", res, x2, [])

            tp.part = "rear"
            k, bk, fr = tp.bank()
            tp.do("pe", "turn_w", ["comb"] + fr, lambda: last(nc.tensor.transpose(
                bk[0:8, t * P:(t + 1) * P], comb[:, t, :], ident[:, :]) for t in range(B)))
            tp.do("act", "turned_w", ["turn_w", ("bias", 1)], lambda: nc.scalar.copy(combT[0:8, :], bk[0:8, :]))
            tp.free(k, "turned_w")

            def up(e):
                s = e % 4
                for m in range(4):
                    k, bk, fr = tp.bank()
                    tp.do("pe", f"up_e{e}_{m}", ["turned3", f"wdn{e}"] + fr, lambda: nc.tensor.matmul(
                        bk, w_in[:, s, m * P:(m + 1) * P], x3T.rearrange("p b t -> p (b t)"), start=True, stop=True))
                    tp.do("act", f"gelu_e{e}_{m}", [f"up_e{e}_{m}", f"down_e{e - 2}" if e >= 2 else (f"down_e{e + 6}", 1)],
                          lambda: nc.scalar.activation(h_exp[:, (e % 2) * 4 + m, :], bk, ACT.Gelu,
                                                       bias=late["b_in"][:, 4 * e + m:4 * e + m + 1]))
                    tp.free(k, f"gelu_e{e}_{m}")
                tp.where[f"up_e{e}"] = tp.where[f"up_e{e}_3"]

            def down(e):
                s = e % 4
                k, bk, fr = tp.bank()
                tp.do("pe", f"down_e{e}", [f"gelu_e{e}_3"] + fr, lambda: last(mms(
                    [(bk[:, t * P:(t + 1) * P], h_exp[:, (e % 2) * 4 + m, t * P:(t + 1) * P], w_dn[:, s, m, :])
                     for m in range(4)]) for t in range(B)))
                tp.do("dve", f"combine{e}", [f"down_e{e}", f"combine{e - 1}" if e else "start"], lambda: last(
                    nc.vector.scalar_tensor_tensor(out=acc[:, t, :], in0=bk[:, t * P:(t + 1) * P],
                                                   scalar=comb[:, t, e:e + 1], in1=acc[:, t, :],
                                                   op0=ALU.mult, op1=ALU.add) for t in range(B)))
                tp.free(k, f"combine{e}")
                if e < 4:
                    load_expert(tp, e + 4)

            up(0)
            k, bk, fr = tp.bank()
            tp.do("pe", "bias", ["turned_w"] + fr, lambda: last(nc.tensor.matmul(
                bk[:, t * P:(t + 1) * P], combT[0:8, t * P:(t + 1) * P], late["b_dn"][0:8, :], start=True, stop=True)
                for t in range(B)))
            tp.do("dve", "start", ["bias", ("norm4", 1)], lambda: nc.vector.tensor_tensor(
                acc, bk.rearrange("p (b c) -> p b c", b=B), x3, ALU.add))
            tp.free(k, "start")
            for e in range(NE):
                if e + 1 < NE:
                    up(e + 1)
                down(e)
                if e == 1:
                    tp.part = "front"
                    turned(tp, 2, x2, x2T, ["v1", "projb9"])
                    tp.part = "rear"
            layernorm(tp, 4, "combine7", acc, x3, ["start"])
            tp.do("act", "stored", ["norm4"], lambda: nc.scalar.dma_start(
                out_v[bass.ds(c, 1)].rearrange("c p b k -> p (c b) k"), x3), line="out")
            tp.pad_banks()

        def load_expert(tp, e):
            s = e % 4
            free = f"down_e{e - 4}" if e >= 4 else (f"down_e{e + 4}", 1)
            tp.do("sp", f"win{e}", [free], lambda: nc.sync.dma_start(w_in[:, s, :], a["w_in"][e]), line=f"we{s}")
            tp.do("sp", f"wdn{e}", [], lambda: nc.sync.dma_start(w_dn[:, s, :, :], a["w_dn"][e]), line=f"we{s}")

        def rear(e, me):
            left = {"pe": [(s_pv, NG * NU)], "act": [(s_exp, NS * NU)], "dve": [(s_ta, QC * NU)],
                    "pool": [(s_att[q], 16 * HQ * NU) for q in range(QC)] + [(s_va, NU)], "sp": [(s_late, 16 * len(LATE))]}
            for s, v in left[me]:
                e.wait_ge(s, v)
            e.sem_inc(s_off, 1)
            e.wait_ge(s_off, 5)
            if me == "pool":
                nc.gpsimd.memset(minus_half, -0.5).then_inc(s_init, 1)
                nc.gpsimd.memset(state.rearrange("p a b c d -> p (a b c d)"), 0.0).then_inc(s_init, 1)
                for i in range(2):
                    nc.gpsimd.memset(k_one[i].rearrange("p a b -> p (a b)"), 0.0).then_inc(s_init, 1)
            e.wait_ge(s_init, 13)
            dry = Tape(None, me, 0, {"front", "rear"}, None)
            body(dry)

            def run(it, live):
                tp = Tape(e, me, it, live, dry)
                body(tp)
                tp.flush()
            run(0, {"front"})
            with e.Fori(1, NITER - 1) as it:
                run(it, {"front", "rear"})
            run(NITER - 1, {"rear"})
            if me == "act":
                e.wait_ge(s_line["out"], 16 * NITER)

        @block.sync
        def _(e):
            for dst, src in ((wqkv[:, :], a["w_qkv"]), (ident[:, :], a["ident"]), (pe_[:, 0, 0:P], a["mask_qk"]),
                             (pe_[:, 1, 0:P], a["mask_kq"])):
                e.dma_start(dst, src).then_inc(s_w, 16)

            def chunk(b, p, first):
                if not first:
                    e.wait_ge(s_proj, 3 * (2 * b + p - 1))
                e.dma_start(xT[:, p, :], a["xT"][:, bass.ds(b * T + p * 512, 512)]).then_inc(s_xT[p], 16)

            def store(b, p):
                e.wait_ge(s_q2, 2 * (2 * b + p) + 2)
                e.wait_ge(s_q3, 2 * (2 * b + p) + 2)
                for w, dst in ((0, q_dst), (1, k_dst)):
                    for r in range(PARTS):
                        e.dma_start(dst[b, r, :, :, p * 512:(p + 1) * 512],
                                    qk3[p][w][:, r, :]).then_inc(s_sc[p], 16)

            chunk(0, 0, True)
            chunk(0, 1, True)
            for p in range(2):
                chunk(1, p, False)
                store(0, p)

            def stacks(u, p, half):
                cols = slice(512 * half, 512 * half + 512)
                for r in range(PARTS):
                    rows = slice(r * PARTS * D0, (r + 1) * PARTS * D0)
                    e.dma_start(sq[p][rows, :, cols], q_parts[u, :, :, cols].rearrange("h r t -> r h t"))\
                        .then_inc(s_st[p][half], 16)
                    for i in range(PARTS):
                        rows = slice((r * PARTS + i) * D0, (r * PARTS + i + 1) * D0)
                        e.dma_start(sk[p][rows, :, cols], k_parts[u, :, r, :, cols].rearrange("h d t -> d h t"))\
                            .then_inc(s_st[p][half], 16)

            def max_rows(u, p):
                e.wait_ge(s_itc, NI * (u + 1))
                for h in range(HQ):
                    e.dma_start(sq[p][MROW:MROW + PARTS, h, :], mrows[h * PARTS:(h + 1) * PARTS, :])\
                        .then_inc(s_mrow, 16)

            e.wait_ge(s_init, 9)
            for p in range(2):
                e.wait_ge(s_sc[p], 16 * 6)
            for half in range(2):
                stacks(0, 0, half)

            def body(b):
                for p in range(2):
                    chunk(b + 1, p, False)
                    store(b, p)
            with_loop(e, 1, B - 1, body)
            for p in range(2):
                store(B - 1, p)
            for half in range(2):
                stacks(1, 1, half)
            for n in LATE:
                e.dma_start(late[n][:], a[n]).then_inc(s_late, 16)
            max_rows(0, 0)
            for p in range(2):
                e.wait_ge(s_sc[p], 16 * 6 * B)

            def unit(u, p, first, last, i):
                more = not (isinstance(u, int) and u >= NU - 2)
                if more:
                    e.wait_ge(s_qk, NS * u + FIRST_STEP[HALF_GROUP])
                    stacks(u + 2, p, 0)
                if not last:
                    max_rows(u + 1, 1 - p)
                if more:
                    e.wait_ge(s_qk, NS * (u + 1))
                    stacks(u + 2, p, 1)
            units(e, unit)
            rear(e, 'sp')

        @block.tensor
        def _(e):
            e.wait_ge(s_w, 16 * 4)

            def chunk(b, p, first):
                e.wait_ge(s_xT[p], 16 * (b + 1))
                if not first:
                    n = 2 * b + p - 1
                    e.wait_ge(s_r1, 2 * n)
                    e.wait_ge(s_v, n)
                for w in range(2):
                    nc.tensor.matmul(banks[:, 4 * p + w, :], wqkv[:, w * C:(w + 1) * C], xT[:, p, :],
                                     start=True, stop=True).then_inc(s_proj, 1)
                for t in range(4):
                    mm_ = nc.tensor.matmul(banks[:, 4 * p + 2, t * P:(t + 1) * P], xT[:, p, t * P:(t + 1) * P],
                                           wqkv[:, 2 * C:3 * C], start=True, stop=True)
                mm_.then_inc(s_proj, 1)
            for p in range(2):
                chunk(0, p, True)
            with_loop(e, 1, B, lambda b: [chunk(b, p, False) for p in range(2)])
            e.wait_ge(s_r1, 4 * B)
            e.wait_ge(s_v, 2 * B)

            def item(u, p, k, i=None):
                qt, hs, k0, n = ITEMS[k]
                if k == 0:
                    e.wait_ge(s_st[p][0], 16 * 12 * (i + 1))
                if k == HALF_ITEM:
                    e.wait_ge(s_st[p][1], 16 * 12 * (i + 1))
                if not (isinstance(u, int) and u == 0 and k < 2):
                    e.wait_ge(s_itc, NI * u + k - 1)
                for at, h in enumerate(hs):
                    col = at * n if len(hs) == 4 else at * 512
                    dst = pair[k % 2].rearrange("p a c -> p (a c)")[:, col:col + n]
                    diag = k0 + n > qt * P
                    ins = nc.tensor.matmul(dst, sq[p][0:MROW, h, qt * P:(qt + 1) * P], sk[p][0:MROW, h, k0:k0 + n],
                                           start=True, stop=not diag, skip_group_check=True)
                    if diag:
                        ins = nc.tensor.matmul(dst[:, n - P:n], identb[:, :], mask_qk[:, :],
                                               start=False, stop=True, skip_group_check=True)
                ins.then_inc(s_it, 1)

            def turn_max(u):
                k = NI - 1
                e.wait_ge(s_m3, u + 1)
                e.wait_ge(s_itc, NI * u + k - 1)
                dst = pair[k % 2].rearrange("p a c -> p (a c)").bitcast(BF16)
                for qt in range(KT):
                    ins = nc.tensor.transpose(dst[0:HQ * PARTS, qt * P:(qt + 1) * P],
                                              m3[:, qt, :, :].rearrange("p h r -> p (h r)"), identb[:, :])
                ins.then_inc(s_it, 1)

            def scores(u, p, steps):
                for s in steps:
                    if not (isinstance(u, int) and u == 0 and s < NBANK):
                        e.wait_ge(s_exp, NS * u + s - NBANK + 1)
                    bank = score[s % NBANK]
                    for h, kt, q0, n, at in STEPS[s]:
                        ins = nc.tensor.matmul(bank[:, at:at + n], sk[p][0:MROW + PARTS, h, kt * P:(kt + 1) * P],
                                               sq[p][0:MROW + PARTS, h, q0:q0 + n], start=True, stop=True,
                                               skip_group_check=True)
                    ins.then_inc(s_qk, 1)

            def times_v(u, p, g):
                qc, steps = GROUPS[g]
                if g == 0:
                    e.wait_ge(s_va, u + 1)
                if g in (0, 3) and not (isinstance(u, int) and u == 0 and g == 0):
                    e.wait_ge(s_t1, QC * u + qc)
                if g in DIAGONAL:
                    e.wait_ge(s_tri, len(DIAGONAL) * u + DIAGONAL.index(g) + 1)
                else:
                    e.wait_ge(s_exp, NS * u + FIRST_STEP[g] + len(steps))
                pieces = sorted(((h, i, pc) for i, st in enumerate(steps) for pc in [st] for h in {x[0] for x in st}))
                done = []
                for rank in range(2):
                    for h in range(HQ):
                        mine = [(FIRST_STEP[g] + i, x) for i, st in enumerate(steps) for x in st if x[0] == h]
                        if rank < len(mine):
                            s, (_, kt, q0, n, at) = mine[rank]
                            lo = q0 - 512 * qc
                            last = g + 1 == NG or GROUPS[g + 1][0] != qc
                            done.append(nc.tensor.matmul(
                                pv_bank[32 * h:32 * h + 32, lo:lo + n], va[p][:, kt, h, :],
                                pe_[:, s % NSLOT, at:at + n], start=(g in (0, 3)), stop=last,
                                skip_group_check=True))
                done[-1].then_inc(s_pv, 1)

            e.wait_ge(s_cst, 3)
            for k in range(NI - 1):
                item(0, 0, k, 0)
            turn_max(0)

            def unit(u, p, first, last, i):
                for g in range(NG):
                    if g == 0:
                        e.wait_ge(s_mrow, 16 * HQ * (u + 1))
                    steps = range(FIRST_STEP[g], FIRST_STEP[g] + len(GROUPS[g][1]))
                    items = [] if last else list(range(PER_SLOT * g, min(PER_SLOT * g + PER_SLOT, NI - 1)))
                    for n in range(2):
                        scores(u, p, steps[2 * n:2 * n + 2])
                        if items:
                            item(u + 1, 1 - p, items.pop(0), i + p)
                    if g or not first:
                        times_v(*((u, p, g - 1) if g else (u - 1, 1 - p, NG - 1)))
                    for k in items:
                        item(u + 1, 1 - p, k, i + p)
                    if not last and g == CHAIN_SLOT:
                        turn_max(u + 1)
            units(e, unit)
            times_v(NU - 1, 1, NG - 1)
            rear(e, 'pe')

        @block.scalar
        def _(e):
            def chunk(b, p, first):
                n = 2 * b + p
                for w in range(2):
                    e.wait_ge(s_proj, 3 * n + w + 1)
                    if not first:
                        e.wait_ge(s_sc[p], 16 * 6 * b)
                    nc.scalar.copy(qk3[p][w][:, 0, :], banks[:, 4 * p + w, :]).then_inc(s_q1, 1)
                for w in range(2):
                    e.wait_ge(s_r1, 2 * n + w + 1)
                    nc.scalar.copy(qk3[p][w][:, 1, :], rest[:, w, :]).then_inc(s_q2, 1)
            for p in range(2):
                chunk(0, p, True)
            with_loop(e, 1, B, lambda b: [chunk(b, p, False) for p in range(2)])

            def unit(u, p, first, last, i):
                for s in range(NS):
                    e.wait_ge(s_qk, NS * u + s + 1)
                    if not (isinstance(u, int) and u == 0 and s < NSLOT):
                        prev = (s - NSLOT) % NS
                        e.wait_ge(s_pv, NG * (u if s >= NSLOT else u - 1) + GROUP_OF[prev] + 1)
                    nc.scalar.activation(pe_[:, s % NSLOT, :], score[s % NBANK], ACT.Exp, scale=SCALE0)\
                        .then_inc(s_exp, 1)
            units(e, unit)
            rear(e, 'act')

        @block.vector
        def _(e):
            e.wait_ge(s_w, 16 * 4)
            for dst, src in ((identb, ident[:, :]), (mask_qk, pe_[:, 0, 0:P]), (mask_kq, pe_[:, 1, 0:P])):
                nc.vector.tensor_copy(dst[:, :], src).then_inc(s_cst, 1)

            def chunk(b, p, first):
                n = 2 * b + p
                for w in range(2):
                    e.wait_ge(s_q1, 2 * n + w + 1)
                    if not (first and p == 0):
                        e.wait_ge(s_q3, 2 * n + w - 1)
                        e.wait_ge(s_q2, 2 * n + w - 1)
                    nc.vector.tensor_tensor(rest[:, w, :], banks[:, 4 * p + w, :], qk3[p][w][:, 0, :], ALU.subtract)\
                        .then_inc(s_r1, 1)
                e.wait_ge(s_proj, 3 * n + 3)
                nc.vector.tensor_copy(
                    vnat[:, bass.ds(4 * b, 4), 4 * p:4 * p + 4, :].rearrange("p j t c -> p t j c"),
                    banks[:, 4 * p + 2, :].rearrange("p (t j c) -> p t j c", t=4, j=4)).then_inc(s_v, 1)
                for w in range(2):
                    e.wait_ge(s_q2, 2 * n + w + 1)
                    nc.vector.tensor_tensor(qk3[p][w][:, 2, :], rest[:, w, :], qk3[p][w][:, 1, :], ALU.subtract)\
                        .then_inc(s_q3, 1)
            for p in range(2):
                chunk(0, p, True)
            with_loop(e, 1, B, lambda b: [chunk(b, p, False) for p in range(2)])
            e.wait_ge(s_init, 9)

            def top(u, k):
                qt, hs, k0, n = ITEMS[k]
                e.wait_ge(s_it, NI * u + k + 1)
                src = pair[k % 2].rearrange("p a c -> p (a c)")
                if len(hs) == 4:
                    src = src[:, 0:4 * n].rearrange("p (h c) -> p h c", c=n)
                else:
                    src = pair[k % 2][:, :, 0:n]
                nc.vector.tensor_reduce(mx[:, 1 if k0 else 0, qt, hs[0]:hs[-1] + 1], src, AX.X, ALU.max)\
                    .then_inc(s_itc, 1)

            def chain(u):
                e.wait_ge(s_itc, NI * u + NI - 1)
                if not (isinstance(u, int) and u == 0):
                    e.wait_ge(s_it, NI * u)
                nc.vector.tensor_tensor(mm, mx[:, 0, :, :], mx[:, 1, :, :], ALU.max).then_inc(s_m, 1)
                e.wait_ge(s_m, 5 * u + 1)
                nc.vector.tensor_scalar(m3[:, :, :, 0], mm, -1.0, None, ALU.mult).then_inc(s_m, 1)
                e.wait_ge(s_m, 5 * u + 2)
                nc.vector.scalar_tensor_tensor(out=mr, in0=mm, scalar=-1.0, in1=m3[:, :, :, 0],
                                               op0=ALU.mult, op1=ALU.subtract).then_inc(s_m, 1)
                e.wait_ge(s_m, 5 * u + 3)
                nc.vector.tensor_copy(m3[:, :, :, 1], mr).then_inc(s_m, 1)
                e.wait_ge(s_m, 5 * u + 4)
                nc.vector.tensor_tensor(m3[:, :, :, 2], mr, m3[:, :, :, 1], ALU.subtract).then_inc(s_m3, 1)
                e.sem_inc(s_m, 1)

            def rows(u):
                k = NI - 1
                e.wait_ge(s_it, NI * u + k + 1)
                if not (isinstance(u, int) and u == 0):
                    e.wait_ge(s_mrow, 16 * HQ * u)
                nc.vector.tensor_copy(mrows[0:HQ * PARTS, :], pair[k % 2].rearrange("p a c -> p (a c)").bitcast(BF16)[0:HQ * PARTS, 0:T])\
                    .then_inc(s_itc, 1)

            def norm(u, qc):
                n = QC * u + qc
                e.wait_ge(s_pv, NG * u + (3 if qc == 0 else NG))
                nc.vector.transpose(tq.rearrange("p a c -> p (a c)"), pv_bank).then_inc(s_t1, 1)
                yield
                e.wait_ge(s_t1, n + 1)
                nc.vector.reciprocal(rl, tq[:, :, D0:D0 + 1]).then_inc(s_n, 1)
                yield
                e.wait_ge(s_n, 2 * n + 1)
                nc.vector.tensor_tensor(tq[:, :, 0:D0], tq[:, :, 0:D0], rl.to_broadcast([P, 16, D0]), ALU.mult)\
                    .then_inc(s_n, 1)
                yield
                e.wait_ge(s_n, 2 * n + 2)
                if not (isinstance(u, int) and u == 0):
                    e.wait_ge(s_att[qc], 16 * HQ * u)
                nc.vector.transpose(ta[:, qc, :], tq.rearrange("p a c -> p (a c)")).then_inc(s_ta, 1)

            for k in range(NI - 1):
                top(0, k)
            chain(0)
            rows(0)

            def unit(u, p, first, last, i):
                pending = iter(())
                for g in range(NG):
                    if g == 0 and not first:
                        pending = norm(u - 1, 1)
                    if g == 3:
                        pending = norm(u, 0)
                    items = [] if last else list(range(PER_SLOT * g, min(PER_SLOT * g + PER_SLOT, NI - 1)))
                    for n, k in enumerate(items):
                        top(u + 1, k)
                        if (g, n) not in ((0, 0), (3, 0), (3, 1)):
                            next(pending, None)
                    if not items:
                        for _ in pending:
                            pass
                    if not last and g == CHAIN_SLOT:
                        chain(u + 1)
                        rows(u + 1)
            units(e, unit)
            for _ in norm(NU - 1, 1):
                pass
            rear(e, 'dve')


        @block.gpsimd
        def _(e):
            for p in range(2):
                nc.gpsimd.memset(sq[p], 0.0).then_inc(s_init, 1)
                nc.gpsimd.memset(sk[p], 0.0).then_inc(s_init, 1)
                nc.gpsimd.memset(va[p], 1.0).then_inc(s_init, 1)
            nc.gpsimd.memset(mx, -3.0e38).then_inc(s_init, 1)
            e.wait_ge(s_init, 7)
            for p in range(2):
                nc.gpsimd.memset(sk[p][MROW:MROW + PARTS, :, :], 1.0).then_inc(s_init, 1)
            e.wait_ge(s_init, 9)

            e.wait_ge(s_v, 2 * B)

            def lay_v(u, p):
                if not (isinstance(u, int) and u < 2):
                    e.wait_ge(s_pv, NG * (u - 1))
                nc.gpsimd.tensor_copy(va[p][:, :, :, 0:D0],
                                      vnat[:, bass.ds(u, 1), :, :].rearrange("p u t (h d) -> p (u t) h d", h=HQ))\
                    .then_inc(s_va, 1)
            lay_v(0, 0)
            lay_v(1, 1)

            def triangle(u, g):
                steps = GROUPS[g][1]
                first_slot = FIRST_STEP[g] % NSLOT
                places = sorted({x[4] for x in steps[0] if x[1] * P == x[2]})
                e.wait_ge(s_exp, NS * u + FIRST_STEP[g] + len(steps))
                e.sem_inc(s_hold, 1)
                flat = pe_.rearrange("p s c -> p (s c)")[:, 512 * first_slot:512 * (first_slot + len(steps))]
                blocks = flat.rearrange("p (s c) -> p s c", c=P)
                if places == [0, 256]:
                    views = [blocks[:, 0:4 * len(steps):2, :]]
                else:
                    views = [blocks[:, at // P:4 * len(steps):4, :] for at in places]
                for v in views:
                    ins = nc.gpsimd.affine_select(out=v, in_=v, compare_op=ALU.is_ge, fill=0.0, base=0,
                                                  pattern=[[0, v.shape[1]], [1, P]], channel_multiplier=-1)
                ins.then_inc(s_tri, 1)

            def unit(u, p, first, last, i):
                def store(v, qc):
                    e.wait_ge(s_ta, QC * v + qc + 1)
                    for h in range(HQ):
                        e.dma_start(att_t[v, h, :, qc * 512:(qc + 1) * 512], ta[32 * h:32 * h + D0, qc, :])\
                            .then_inc(s_att[qc], 16)
                for g in range(NG):
                    if g in DIAGONAL:
                        triangle(u, g)
                    if g == 1 and not first:
                        store(u - 1, 1)
                    if g == 5:
                        store(u, 0)
                        if not first and not last:
                            lay_v(u + 1, 1 - p)
                if last:
                    store(u, 1)
            units(e, unit)
            rear(e, 'pool')


def layouts(x):
    a = {}
    f32 = np.float32
    a["xT"] = x["L0_attn_x"].reshape(NT, C).T
    a["x"] = x["L0_attn_x"]
    a["w_qkv"] = x["L0_attn_w_qkv"]
    a["wo0"] = x["L0_attn_w_out"]
    a["w1"], a["w2"] = x["L0_ffn_w1_w"].T, x["L0_ffn_w2_w"].T
    a["h1"], a["h2"], a["w3"] = (x[f"L0_ffn_{n}_w"].T.reshape(4, P, -1).transpose(1, 0, 2) for n in ("h1", "h2", "w3"))
    a["s1"], a["s2"], a["sh1"], a["sh2"] = (x[f"L0_ffn_{n}_s"].reshape(4, P).T for n in ("w1", "w2", "h1", "h2"))
    a["s3"] = np.broadcast_to(x["L0_ffn_w3_s"], (P, C))
    order = np.array([[4 * (2 * kp + g) + i for g in range(2)] for kp in range(2) for i in range(4)])
    swap = (np.arange(D1) + D1 // 2) % D1
    wq = x["L1_attn_Wq"].reshape(H1, D1, C)
    wk = x["L1_attn_Wk"].reshape(KV1, D1, C)
    a["wq"], a["wqr"] = (w[order].reshape(8, P, C).transpose(2, 0, 1) for w in (wq, wq[:, swap]))
    a["wk"], a["wkr"] = (w.reshape(2, P, C).transpose(2, 0, 1) for w in (wk, wk[:, swap]))
    a["wv"] = x["L1_attn_Wv"].T
    a["wo1"] = x["L1_attn_Wo"].T.reshape(H1, D1, C)[order].reshape(8, P, C).transpose(1, 0, 2)
    inv = 1.0 / 10000.0 ** (np.arange(0, D1, 2, dtype=np.float64) / D1)
    ang = np.outer(np.arange(T, dtype=np.float64), inv)
    ang = np.concatenate([ang, ang], axis=1).T
    sign = np.where(np.arange(D1) < D1 // 2, -1.0, 1.0)[:, None]
    a["cos"] = np.tile(np.cos(ang), (2, 1)).astype(f32)
    a["sin"] = np.tile(np.sin(ang) * sign, (2, 1)).astype(f32)
    slope = np.array([2.0 ** (-8.0 / H1 * (i + 1)) for i in range(H1)], f32).astype(np.float64)
    t = np.arange(P, dtype=np.float64)
    gap = t[None, :] - t[:, None]
    a["mask1"] = np.stack([np.where(gap >= 0, np.exp(-sl * np.maximum(gap, 0)), 0.0) for sl in slope], 1)\
        .reshape(P, H1 * P).astype(f32)
    a["qdec"] = np.exp(-slope[order][:, :, None] * (t + 1.0)).repeat(D1, 1).transpose(1, 0, 2).astype(f32)
    a["kdec"] = np.exp(-slope[None, :] * (P - 1.0 - t)[:, None]).astype(f32)
    a["bdec"] = np.exp(-slope[order] * P).repeat(D1, 1).T.astype(f32)
    a["wgate"] = x["L1_ffn_W_gate"]
    a["w_in"] = x["L1_ffn_W_in"]
    a["b_in"] = x["L1_ffn_b_in"].reshape(8, 4, P).transpose(2, 0, 1).reshape(P, 32)
    a["w_dn"] = x["L1_ffn_W_out"].reshape(8, 4, P, C).transpose(0, 2, 1, 3)
    a["b_dn"] = x["L1_ffn_b_out"]
    a["iota"] = np.broadcast_to(np.arange(8, dtype=f32), (P, 8))
    eye = np.eye(P, dtype=np.float32)
    a["ident"] = eye
    upper = np.where(np.arange(P)[:, None] >= np.arange(P)[None, :], 0.0, NEG)
    a["mask_qk"] = upper.astype(f32)
    a["mask_kq"] = upper.T.astype(f32)
    return {k: np.ascontiguousarray(v) for k, v in a.items()}


def kernel(**inputs):
    import concourse.bacc as bacc
    from concourse.bass_utils import run_bass_kernel_spmd

    nc = bacc.Bacc("TRN2", target_bir_lowering=False, num_devices=1)
    arrays = layouts({k: np.asarray(v) for k, v in inputs.items()})
    aps = {k: nc.dram_tensor(f"in_{k}", v.shape, mybir.dt.from_np(v.dtype), kind="ExternalInput").ap()
           for k, v in arrays.items()}
    out = nc.dram_tensor("out_0", (B, T, C), F32, kind="ExternalOutput").ap()
    program(nc, aps, out)
    r = run_bass_kernel_spmd(nc, [{f"in_{k}": v for k, v in arrays.items()}], core_ids=[0])
    return r.results[0]["out_0"]
```

```python
from contextlib import ExitStack

import numpy as np

import concourse.bass as bass
from concourse import mybir

F32 = mybir.dt.float32
BF16 = mybir.dt.bfloat16
U32 = mybir.dt.uint32
ALU = mybir.AluOpType
ACT = mybir.ActivationFunctionType
AX = mybir.AxisListType

P = 128
B, T, C = 4, 1024, 128
NT = B * T
EPS = 1e-5

H0, D0 = 16, 8
HQ = 4
NU = B * (H0 // HQ)
KT = T // P
QC = T // 512
PARTS = 3
SROWS = PARTS * PARTS * D0
MROW = 96
SCALE0 = float(D0) ** -0.5
NEG = -1.0e30
NBANK = 3
NSLOT = 12


def exp_plan():
    groups = []
    for qc in range(QC):
        q0 = 512 * qc
        for kt in range(4 * qc + 1):
            groups.append((qc, [[(h, kt, q0, 512, 0)] for h in range(HQ)]))
        a = 4 * qc
        groups.append((qc, [[(h, a + 1, q0 + 128, 384, 0), (h, a + 3, q0 + 384, 128, 384)] for h in range(HQ)]))
        groups.append((qc, [[(h, a + 2, q0 + 256, 256, 256 * (h % 2)) for h in (g, g + 1)] for g in (0, 2)]))
    return groups


def max_plan():
    items = []
    for qt in range(KT):
        for k0 in range(0, P * (qt + 1), 512):
            n = min(512, P * (qt + 1) - k0)
            whole = n == P or (n == 256 and k0)
            items += [(qt, hs, k0, n) for hs in ([range(4)] if whole else [range(2), range(2, 4)])]
    return items


GROUPS = exp_plan()
NG = len(GROUPS)
STEPS = [s for _, g in GROUPS for s in g]
NS = len(STEPS)
DIAGONAL = [g for g, (_, st) in enumerate(GROUPS) if any(x[2] == x[1] * P for y in st for x in y)]
GROUP_OF = [g for g, (_, steps) in enumerate(GROUPS) for _ in steps]
HALF_GROUP = 1 + max(g for g, (_, st) in enumerate(GROUPS) if any(min(x[1] * P, x[2]) < 512 for y in st for x in y))
FIRST_STEP = [GROUP_OF.index(g) for g in range(NG)]
ITEMS = max_plan()
NI = len(ITEMS) + 1
HALF_ITEM = min(k for k, (qt, _, _, _) in enumerate(ITEMS) if qt >= 4)
PER_SLOT = 3
assert NS % NBANK == 0 and NS % NSLOT == 0 and NI % 2 == 0
CHAIN_SLOT = -(-len(ITEMS) // PER_SLOT)
assert CHAIN_SLOT + 1 < NG


H1, KV1, D1 = 16, 4, 64
LATE = ["wo0", "w1", "w2", "h12", "w3", "s1", "s2", "sh1", "sh2", "s3", "wq", "wk", "wv", "wo1",
        "mask1", "qdec", "kdec", "bdec", "wgate", "b_in", "b_dn", "iota",
        "before", "token", "region", "upto", "multiples", "number"]
ARENA = 40128

NE, TOPK = 8, 2
REGION = NT + P
NTILE = TOPK * NT // P + NE
ROW = C + 2
XG = 8
assert NTILE % XG == 0


def program(nc, a, out):
    with ExitStack() as ctx:
        def sb(name, shape, dt=F32):
            return ctx.enter_context(nc.sbuf_tensor(name, shape, dt))

        def sem(name):
            return ctx.enter_context(nc.semaphore(name))

        banks = ctx.enter_context(nc.psum_tensor("banks", [P, 8, 512], F32))
        q_parts = nc.dram_tensor("q_parts", [NU, HQ, PARTS * D0, T], BF16, kind="Internal").ap()
        k_parts = nc.dram_tensor("k_parts", [NU, HQ, PARTS, D0, T], BF16, kind="Internal").ap()
        rows = nc.dram_tensor("rows", [NE * REGION + NE * P, ROW], F32, kind="Internal").ap()
        best = nc.dram_tensor("best", [TOPK * NT + 2 * NE * P, C], F32, kind="Internal").ap()
        rest_d = nc.dram_tensor("rest_d", [T // P, P, B, C], F32, kind="Internal").ap()
        att_t = nc.dram_tensor("att_t", [NU, HQ, D0, T], F32, kind="Internal").ap()

        ident = sb("ident", [P, P])
        identb = sb("identb", [P, P], BF16)
        mask_qk = sb("mask_qk", [P, P], BF16)
        mask_kq = sb("mask_kq", [P, P], BF16)
        wqkv = sb("wqkv", [P, 3 * C])
        late = {n: sb(n, list(a[n].shape)) for n in LATE}

        arena = sb("arena", [P, ARENA])

        def carve():
            at = [0]

            def view(shape, dt=F32):
                n = int(np.prod(shape[1:]))
                words = n if dt == F32 else n // 2
                v = arena[:, at[0]:at[0] + words]
                at[0] += words
                assert at[0] <= ARENA, at
                if dt != F32:
                    v = v.bitcast(dt)
                if len(shape) > 2:
                    names = " ".join("abcd"[:len(shape) - 1])
                    v = v.rearrange(f"p ({names}) -> p {names}", **dict(zip("abcd", shape[1:])))
                return v
            return view

        view = carve()
        vnat = view([P, NU, KT, HQ * D0])
        xT = view([P, 2 * B, 512])
        qk3 = [[view([P, PARTS, 512], BF16) for w in range(2)] for p in range(2)]
        rest = view([P, 2, 512])
        sq = [view([P, HQ, T], BF16) for p in range(2)]
        sk = [view([P, HQ, T], BF16) for p in range(2)]
        va = [view([P, KT, HQ, 32]) for p in range(2)]
        pe_ = view([P, NSLOT, 512])
        mx = view([P, 2, KT, HQ])
        mm = view([P, KT, HQ])
        mr = view([P, KT, HQ])
        m3 = view([P, KT, HQ, PARTS], BF16)
        mrows = view([P, T], BF16)
        tq = view([P, 16, 32])
        rl = view([P, 16, 1])
        ta = view([P, QC, 512])

        CST = 3
        s_cst = sem("s_cst")
        s_w = sem("s_w")
        s_late = sem("s_late")
        s_init = sem("s_init")
        s_xT = [sem(f"s_xT{n}") for n in range(2 * B)]
        s_proj = sem("s_proj")
        s_q1 = sem("s_q1")
        s_r1 = sem("s_r1")
        s_q2 = sem("s_q2")
        s_q3 = sem("s_q3")
        s_v = sem("s_v")
        s_sc = [sem(f"s_sc{p}") for p in range(2)]
        s_sq = [sem(f"s_sq{p}") for p in range(2)]
        s_st = [[sem(f"s_st{p}{half}") for half in range(2)] for p in range(2)]
        s_va = sem("s_va")
        s_qk = sem("s_qk")
        s_exp = sem("s_exp")
        s_tri = sem("s_tri")
        s_hold = sem("s_hold")
        s_pv = sem("s_pv")
        s_it = sem("s_it")
        s_itc = sem("s_itc")
        s_m = sem("s_m")
        s_m3 = sem("s_m3")
        s_mrow = sem("s_mrow")
        s_t1 = sem("s_t1")
        s_n = sem("s_n")
        s_ta = sem("s_ta")
        s_att = [sem(f"s_att{q}") for q in range(QC)]

        block = ctx.enter_context(nc.Block())
        score = [banks[:, i, :] for i in range(NBANK)]
        pv_bank = banks[:, NBANK, :]
        pair = [banks[:, 4 + 2 * i:6 + 2 * i, :] for i in range(2)]
        q_dst = q_parts.rearrange("(b j) h (a d) t -> b a (j h) d t", b=B, a=PARTS)
        k_dst = k_parts.rearrange("(b j) h a d t -> b a (j h) d t", b=B)

        def units(eng, unit):
            for u in range(2):
                unit(u, u % 2, u == 0, False, 0)
            with_loop(eng, 1, NU // 2 - 1, lambda i: [unit(2 * i + p, p, False, False, i) for p in range(2)])
            for u in range(NU - 2, NU):
                unit(u, u % 2, False, u == NU - 1, u // 2)

        def with_loop(eng, lo, hi, body):
            with eng.Fori(lo, hi) as i:
                body(i)

        view = carve()
        q_all = view([P, 8, 512])
        q_dec = view([P, 4, 4, P])
        k_all = view([P, 2, 512])
        k_one = [view([P, 2, 512]) for _ in range(2)]
        rot_ab = view([P, 4096])
        raw, swapped = (rot_ab[:, 2048 * i:2048 * i + 2048].rearrange("p (s n t) -> p s n t", s=2, n=2)
                        for i in range(2))
        v_nat = view([P, B, KV1, D1])
        k_nat = view([P, 2, B, P])
        v_dec = view([P, 2, 2, 4, D1])
        sm = view([P, 4, 512])
        o_t = view([P, 4, 4, P])
        raw = [raw[:, k] for k in range(2)] + [sm[:, 2 * k:2 * k + 2, :] for k in range(2)]
        swapped = [swapped[:, k] for k in range(2)] + \
                  [o_t[:, 2 * k:2 * k + 2].rearrange("p s i t -> p s (i t)") for k in range(2)]
        state = view([P, B, 2, 4, P])
        cos_c, sin_c = view([P, P]), view([P, P])
        att_c = view([P, B, P])
        x_in = view([P, B, P])
        x1, x1T, x2, x2T = (view([P, B, P]) for _ in range(4))
        x3T = x1T
        x3_rows = view([P, TOPK, B, ROW])
        x3 = x3_rows[:, 0, :, 0:C]
        res = view([P, B, P])
        acc = view([P, B, P])
        gated = view([P, 2, 512])
        hid = [view([P, 4, 512]) for _ in range(2)]
        w_in = view([P, NE, 512])
        stats = view([P, B, 8])
        mv = view([P, B, 2])
        var = view([P, B])
        rstd = view([P, B])
        minus_half = view([P, B])
        spare = view([P, 2])
        logit = view([P, B, 8])
        top8 = view([P, B, 8])
        idxf = view([P, B, 8])
        expd = view([P, B])
        wgt = view([P, 2, B])
        chosen = view([P, TOPK * B + 1, NE], BF16)
        below = view([P, P], BF16)
        ones = view([P, P], BF16)
        base = view([P, NE])
        place = view([P, TOPK * B + 1, NE])
        own = view([P, TOPK * B, NE])
        slotf = view([P, TOPK * B])
        sent = view([P, TOPK * B]).bitcast(U32)
        pick = view([P, 2, B, 8])
        comb = view([P, B, 8])
        combT = gated[:, 0, :]
        idx8 = view([P, B, 8]).bitcast(U32)

        NITER = T // P + 2
        w_dn = late["h12"][:, :, :, :].rearrange("p i k m -> p (i k m)").rearrange("p (e m) -> p e m", e=NE)
        b_in = late["b_in"][:, :].rearrange("p (e m) -> p e m", e=NE)
        at_q = [0]

        def reuse(shape):
            n = int(np.prod(shape[1:]))
            v = q_all.rearrange("p a b -> p (a b)")[:, at_q[0]:at_q[0] + n]
            at_q[0] += n
            assert at_q[0] <= 8 * 512
            names = " ".join("abcd"[:len(shape) - 1])
            return v.rearrange(f"p ({names}) -> p {names}", **dict(zip("abcd", shape[1:]))) if len(shape) > 2 else v
        x_g, y_g = reuse([P, XG, ROW]), reuse([P, XG, C])
        x_gT, h_g = reuse([P, 4, P]), reuse([P, 2, 512])
        mv_e, st_e = reuse([P, T // P, B, 2]), reuse([P, T // P, B, 8])
        var_e, rstd_e, less_e = (reuse([P, T // P, B]) for _ in range(3))
        at_q = [0]

        def reuse_k(shape):
            n = int(np.prod(shape[1:]))
            v = rot_ab[:, at_q[0]:at_q[0] + n]
            at_q[0] += n
            assert at_q[0] <= 2048
            names = " ".join("abcd"[:len(shape) - 1])
            return v.rearrange(f"p ({names}) -> p {names}", **dict(zip("abcd", shape[1:]))) if len(shape) > 2 else v
        table = reuse_k([P, 2 * NTILE + NE]).bitcast(U32)
        t_count, t_tiles, t_cum = (reuse_k([P, NE]) for _ in range(3))
        t_cmp, t_sq, t_ge = reuse_k([P, NE, T * B // P]), reuse_k([P, NE, NE]), reuse_k([P, NTILE, NE])
        t_expert, t_skip, t_row = (reuse_k([P, NTILE]) for _ in range(3))
        STEPS_TAB = 16
        w_now = hid[0][:, 0:4, :]
        halves = [q_dec.rearrange("p a b t -> p (a b t)"), o_t.rearrange("p a b t -> p (a b t)"),
                  sm.rearrange("p a t -> p (a t)"), hid[1].rearrange("p a t -> p (a t)")]

        def quarter(x, k):
            return x[:, 512 * k:512 * k + 512].rearrange("p (b t) -> p b t", b=B)
        parts = [(quarter(state.rearrange("p b k i t -> p (b k i t)"), k), quarter(halves[k // 4], k % 4),
                  quarter(halves[2 + k // 4], k % 4)) for k in range(T // P)]
        best_v = best[0:TOPK * NT, :].rearrange("(r b c p) k -> r c p b k", r=TOPK, b=B, p=P)
        s_experts = sem("s_experts")
        s_pad = sem("s_pad")
        s_tab = sem("s_tab")
        s_xg = [sem(f"s_xg{k}") for k in range(XG)]
        s_w1 = sem("s_w1")
        s_tp, s_xt = sem("s_tp"), sem("s_xt")
        s_up, s_gelu = sem("s_up"), sem("s_gelu")
        s_down, s_y = sem("s_down"), sem("s_y")
        s_back = [sem(f"s_back{k}") for k in range(XG)]
        s_rest = sem("s_rest")
        s_parts = [sem(f"s_parts{k}") for k in range(T // P)]
        s_both, s_d, s_var4 = sem("s_both"), sem("s_d"), sem("s_var4")
        s_rstd4, s_norm = sem("s_rstd4"), sem("s_norm")
        s_out = sem("s_result")
        x_v = a["x"].rearrange("b (c p) k -> c p b k", p=P)
        out_v = out.rearrange("b (c p) k -> c p b k", p=P)
        att_v = att_t.rearrange("(b j) h d t -> (j h d) b t", b=B)
        lines = ["pe", "act", "dve", "pool", "attc", "xin", "rope", "swap0", "swap1", "swap2", "swap3", "scat", "out"]
        s_line = {n: sem(f"s_{n}") for n in lines}
        s_off = sem("s_off")

        class Tape:

            def __init__(self, eng, me, it, live, before):
                self.eng, self.me, self.it, self.live, self.before = eng, me, it, live, before
                self.count = {n: 0 for n in lines}
                self.where = {}
                self.seen = {}
                self.null = 0
                self.held = []
                self.users = [{} for _ in range(8)]
                self.part = None

            def wait(self, need):
                name, ago = (need, 0) if isinstance(need, str) else need
                if ago:
                    if self.before is None:
                        return
                    line, k = self.before.where[name]
                    k -= self.before.count[line]
                else:
                    line, k = self.where[name]
                if self.seen.get(line, -10 ** 6) >= k:
                    return
                self.seen[line] = k
                unit = 1 if line in ("pe", "act", "dve", "pool") else 16
                per = self.before.count[line] if self.before else 0
                value = ((self.it - 2 * (line == "scat")) * per + k) * unit
                if isinstance(value, int) and value <= 0:
                    return
                self.eng.wait_ge(s_line[line], value)
                if self.me == "sp":
                    self.eng.sem_inc(s_hold, 1)

            def flush(self):
                if self.null:
                    per = self.before.count[self.me]
                    done = self.it * per + self.count[self.me] - self.null
                    if done > 0:
                        self.eng.wait_ge(s_line[self.me], done)
                    self.eng.sem_inc(s_line[self.me], self.null)
                    self.null = 0

            def do(self, who, name, needs, fn, line=None, apart=False):
                line = line or who
                unit = 1 if line == who else 16
                if self.me == who and self.eng is not None:
                    if self.part in self.live:
                        self.flush()
                        for n in needs:
                            self.wait(n)
                        if apart:
                            if who == "dve":
                                nc.vector.memset(spare, 0.0)
                            else:
                                self.eng.sem_inc(s_hold, 1)
                        fn().then_inc(s_line[line], unit)
                    elif line == who:
                        self.count[line] += 1
                        self.null += 1
                        self.where[name] = (line, self.count[line])
                        return
                    elif line != "scat":
                        self.eng.sem_inc(s_line[line], 16)
                self.count[line] += 1
                self.where[name] = (line, self.count[line])

            def bank(self):
                k = len(self.held)
                if k >= 8:
                    need = self.held[k - 8]
                elif self.before is None:
                    need = []
                else:
                    need = [(name, 1) for name in self.before.users[k % 8].values()]
                self.held.append(need)
                return k, banks[:, k % 8, :], need

            def free(self, k, name):
                self.held[k] = [name] if self.part in self.live else self.held[k] + [name]
                self.users[k % 8][self.part] = name

            def pad_banks(self):
                while len(self.held) % 8:
                    self.held.append(self.held[len(self.held) - 8])

        def mms(pairs):
            for n, (dst, l, r) in enumerate(pairs):
                ins = nc.tensor.matmul(dst, l, r, start=(n == 0), stop=(n == len(pairs) - 1), skip_group_check=True)
            return ins

        def last(gen):
            for ins in gen:
                pass
            return ins

        def layernorm(tp, tag, need, src, dst, dst_free):
            tp.do("dve", f"stats{tag}", [need], lambda: last(
                nc.vector.bn_stats(stats[:, t, 0:6], src[:, t, :]) for t in range(B)))
            tp.do("dve", f"aggr{tag}", [f"stats{tag}"], lambda: last(
                nc.vector.bn_aggr(mv[:, t, :], stats[:, t, 0:6]) for t in range(B)), apart=True)
            tp.do("dve", f"var{tag}", [f"aggr{tag}"], lambda: nc.vector.tensor_scalar(
                var[:, :], mv[:, :, 1], EPS, None, ALU.add))
            tp.do("pool", f"rstd{tag}", [f"var{tag}"], lambda: nc.gpsimd.tensor_tensor(
                rstd[:, :], var[:, :], minus_half[:, :], ALU.pow))
            tp.do("dve", f"norm{tag}", [f"rstd{tag}"] + dst_free, lambda: last(
                nc.vector.tensor_scalar(dst[:, t, :], src[:, t, :], mv[:, t, 0:1], rstd[:, t:t + 1],
                                        ALU.subtract, ALU.mult) for t in range(B)))

        def turned(tp, tag, src, dst, dst_free, ago=0):
            k, bk, fr = tp.bank()
            tp.do("pe", f"turn{tag}", [(f"norm{tag}", ago)] + fr, lambda: last(
                nc.tensor.transpose(bk[:, t * P:(t + 1) * P], src[:, t, :], ident[:, :]) for t in range(B)))
            tp.do("act", f"turned{tag}", [f"turn{tag}"] + dst_free, lambda: nc.scalar.copy(
                dst.rearrange("p b t -> p (b t)"), bk))
            tp.free(k, f"turned{tag}")

        def body(tp):
            it = tp.it
            c = it - 2

            tp.part = "pre"
            tp.do("sp", "att_in", [("outproj", 1)], lambda: nc.sync.dma_start(
                att_c, att_v[:, :, bass.ds(it * P, P)]), line="attc")
            tp.part = "front"
            tp.do("act", "x1_copy", [("turn1", 1), ("res2", 1)], lambda: nc.scalar.copy(x1, x_in))
            tp.part = "pre"
            tp.do("sp", "x_in", ["x1_copy"], lambda: nc.sync.dma_start(
                x_in, x_v[bass.ds(it, 1)].rearrange("c p b k -> p (c b) k")), line="xin")
            tp.part = "front"
            xt1 = x1T.rearrange("p b t -> p (b t)")
            for m in range(4):
                if m == 2:
                    tp.part = "rear"
                    turned(tp, 2, x2, x2T, [("v1", 1), ("proj4_1", 1)], 1)
                    tp.part = "front"
                k, bk, fr = tp.bank()
                tp.do("pe", f"up_a{m}", [("turned1", 1)] + fr, lambda: nc.tensor.matmul(
                    bk, late["w1"][:, m * P:(m + 1) * P], xt1, start=True, stop=True))
                tp.do("act", f"silu{m}", [f"up_a{m}", f"mul{m - 2}" if m >= 2 else (f"mul{m + 2}", 1), ("bias", 1)],
                      lambda: nc.scalar.activation(gated[:, m % 2, :], bk, ACT.Silu, scale=late["s1"][:, m:m + 1]))
                tp.free(k, f"silu{m}")
                k, bk, fr = tp.bank()
                tp.do("pe", f"up_b{m}", fr, lambda: nc.tensor.matmul(
                    bk, late["w2"][:, m * P:(m + 1) * P], xt1, start=True, stop=True))
                tp.do("dve", f"mul{m}", [f"up_b{m}", f"silu{m}", ("down0", 1)],
                      lambda: nc.vector.scalar_tensor_tensor(
                    out=hid[0][:, m, :], in0=bk, scalar=late["s2"][:, m:m + 1], in1=gated[:, m % 2, :],
                    op0=ALU.mult, op1=ALU.mult))
                tp.free(k, f"mul{m}")

            tp.part = "rear"
            tp.do("sp", "rope", [("turn_b4", 1)], lambda: nc.sync.dma_start(
                cos_c, a["cos"][:, bass.ds(c * P, P)]), line="rope")
            tp.do("sp", "rope2", [], lambda: nc.sync.dma_start(
                sin_c, a["sin"][:, bass.ds(c * P, P)]), line="rope")
            xt = x2T.rearrange("p b t -> p (b t)")
            def home(i, n=2, at=0):
                return (k_all if i == 0 else q_all[:, 2 * i - 2:2 * i, :])[:, at:at + n, :]

            def finish(i):
                sl = i % 4
                both = swapped[sl].rearrange("p n (b t) -> p (n b) t", b=B)
                tp.do("dve", f"turn_b{i}", [f"swap3_{i}"], lambda: nc.vector.tensor_tensor(
                    both, both, sin_c.rearrange("p (o t) -> p o t", o=1).to_broadcast([P, 2 * B, P]), ALU.mult))
                tp.do("pool", f"rotated{i}", [f"turn_b{i}", f"turn_a{i}_1"], lambda: nc.gpsimd.tensor_tensor(
                    home(i), home(i), swapped[sl], ALU.add))
                for n in ((8, 9) if i == 0 else (2 * i - 2, 2 * i - 1)):
                    tp.where[f"rot{n}"] = tp.where[f"rotated{i}"]

            for i in range(5):
                sl = i % 4
                before = {0: (4, 1), 4: (0, 0)}.get(i, (i, 1))
                shared = [("attn7", 1)] if sl >= 2 else []
                if i >= 2:
                    finish(i - 2)
                for n in range(2):
                    w = late["wk"][:, n, :] if i == 0 else late["wq"][:, 2 * i - 2 + n, :]
                    k, bk, fr = tp.bank()
                    tp.do("pe", f"proj{i}_{n}", ["turned2"] + fr, lambda: nc.tensor.matmul(
                        bk, w, xt, start=True, stop=True))
                    tp.do("act", f"raw{i}_{n}", [f"proj{i}_{n}", (f"swap3_{before[0]}", before[1])] + shared,
                          lambda: nc.scalar.copy(raw[sl][:, n, :], bk))
                    used = [("scores_last", 1), ("qdec7", 1)] if i else [("kt_last", 1)]
                    tp.do("dve", f"turn_a{i}_{n}", ["rope2", f"raw{i}_{n}"] + used, lambda: nc.vector.tensor_tensor(
                        home(i, 1, n).rearrange("p o (b t) -> p (o b) t", b=B), bk.rearrange("p (b t) -> p b t", b=B),
                        cos_c.rearrange("p (o t) -> p o t", o=1).to_broadcast([P, B, P]), ALU.mult))
                    tp.free(k, f"turn_a{i}_{n}")
                for h in range(4):
                    to, fro = D1 // 2 * h, D1 // 2 * (h ^ 1)
                    tp.do("sp", f"swap{h}_{i}", [f"raw{i}_1", (f"rotated{before[0]}", before[1])] + [("y3", 1)] * (sl >= 2),
                          lambda: nc.sync.dma_start(swapped[sl][to:to + D1 // 2], raw[sl][fro:fro + D1 // 2]),
                          line=f"swap{sl}")
            for g in range(2):
                k, bk, fr = tp.bank()
                tp.do("pe", f"v{g}", fr, lambda: last(nc.tensor.matmul(
                    bk[:, 256 * i:256 * i + 256], x2T[:, 2 * g + i, :], late["wv"][:, :], start=True, stop=True)
                    for i in range(2)))
                tp.do("act", f"vn{g}", [f"v{g}", ("vdec_last", 1), ("attn_last", 1)], lambda: nc.scalar.copy(
                    v_nat[:, 2 * g:2 * g + 2, :, :].rearrange("p b g d -> p (b g d)"), bk))
                tp.free(k, f"vn{g}")
            def hidden(i, src, dst, need, beside):
                for m in range(4):
                    if m in beside:
                        tp.part = "rear"
                        beside[m]()
                        tp.part = "front"
                    k, bk, fr = tp.bank()
                    tp.do("pe", f"hid{i}_{m}", [need] + fr, lambda: mms(
                        [(bk, late["h12"][:, i - 1, kk, m * P:(m + 1) * P], src[:, kk, :]) for kk in range(4)]))
                    tp.do("act", f"gelu{i}_{m}", [f"hid{i}_{m}"], lambda: nc.scalar.activation(
                        dst[:, m, :], bk, ACT.Gelu, scale=late[f"sh{i}"][:, m:m + 1]))
                    tp.free(k, f"gelu{i}_{m}")
            tp.part = "front"
            hidden(1, hid[0], hid[1], "mul3", {m: (lambda m=m: finish(2 + m)) for m in (1, 2)})
            tp.part = "rear"
            for kp in range(2):
                tp.do("act", f"k_one{kp}", [f"rot{8 + kp}", ("scores_last", 1)], lambda: last(nc.scalar.copy(
                    k_one[i][64 * i:64 * i + 64, kp, :], k_all[64 * i:64 * i + 64, kp, :]) for i in range(2)))
            for kp in range(2):
                k, bk, fr = tp.bank()
                tp.do("pe", f"kt{kp}", [f"rot{8 + kp}"] + fr, lambda: last(nc.tensor.transpose(
                    bk[:, t * P:(t + 1) * P], k_all[:, kp, t * P:(t + 1) * P], ident[:, :]) for t in range(B)))
                tp.do("act", f"kn{kp}", [f"kt{kp}", ("grow_last", 1)], lambda: nc.scalar.copy(
                    k_nat[:, kp, :, :].rearrange("p b d -> p (b d)"), bk))
                tp.free(k, f"kn{kp}")

            def scores1(n):
                b, kp = divmod(n, 2)
                tp.do("pool", f"qdec{n}", [f"rot{4 * kp + 3}", f"attn{n - 4}" if n >= 4 else (f"attn{n + 4}", 1)],
                      lambda: nc.gpsimd.tensor_tensor(
                    q_dec[:, n % 4, :, :], q_all[:, 4 * kp:4 * kp + 4, b * P:(b + 1) * P],
                    late["qdec"][:, 4 * kp:4 * kp + 4, :], ALU.mult))
                tp.do("pool", f"vdec{n}", ["vn1", f"grow{n - 2}" if n >= 2 else (f"grow{n + 6}", 1)],
                      lambda: nc.gpsimd.tensor_tensor(
                    v_dec[:, n % 2, :, :, :].rearrange("p g i d -> p (g i) d"),
                    v_nat[:, b, 2 * kp:2 * kp + 2, :].rearrange("p (g o) d -> p g o d", o=1)
                    .to_broadcast([P, 2, 4, D1]).rearrange("p g i d -> p g i d"),
                    late["kdec"][:, 8 * kp:8 * kp + 8].rearrange("p (g i o) -> p g i o", g=2, o=1)
                    .to_broadcast([P, 2, 4, D1]), ALU.mult))
                for i in range(2):
                    k, bk, fr = tp.bank()
                    s = (2 * n + i) % 4
                    prev = f"attn{n - 2}" if n >= 2 else (f"attn{n + 6}", 1)
                    tp.do("pe", f"scores{n}{i}", [f"k_one{kp}", f"rot{4 * kp + 3}"] + fr, lambda: nc.tensor.matmul(
                        bk, k_one[i][:, kp, b * P:(b + 1) * P], q_all[:, 4 * kp:4 * kp + 4, b * P:(b + 1) * P],
                        start=True, stop=True))
                    tp.do("dve", f"masked{n}{i}", [f"scores{n}{i}", prev, "swap3_2", "swap3_3"], lambda: nc.vector.tensor_tensor(
                        sm[:, s, :], bk, late["mask1"][:, 512 * (2 * kp + i):512 * (2 * kp + i) + 512], ALU.mult))
                    tp.free(k, f"masked{n}{i}")

            def attend(n):
                b, kp = divmod(n, 2)
                k, bk, fr = tp.bank()

                def products():
                    for i in range(2):
                        nc.tensor.matmul(bk[64 * i:64 * i + 64, :], v_nat[:, b, 2 * kp + i, :], sm[:, (2 * n + i) % 4, :],
                                         start=True, stop=False, skip_group_check=True)
                    for i in range(4):
                        ins = nc.tensor.matmul(bk[:, i * P:(i + 1) * P], state[:, b, kp, i, :], q_dec[:, n % 4, i, :],
                                               start=False, stop=True, skip_group_check=True)
                    return ins
                tp.do("pe", f"attn{n}", [f"masked{n}1", f"qdec{n}", (f"state{n}", 1)] + fr, products)
                used = (f"y{n // 2 + 2}", 1) if n < 4 else f"y{n // 2 - 2}"
                tp.do("act", f"o{n}", [f"attn{n}", used, "rotated3"], lambda: nc.scalar.copy(
                    o_t[:, n % 4, :, :].rearrange("p i t -> p (i t)"), bk))
                tp.free(k, f"o{n}")
                k, bk, fr = tp.bank()
                tp.do("pe", f"grow{n}", [f"kn{kp}", f"vdec{n}"] + fr, lambda: last(nc.tensor.matmul(
                    bk[64 * i:64 * i + 64, 0:256], k_nat[:, kp, b, 64 * i:64 * i + 64],
                    v_dec[:, n % 2, i, :, :].rearrange("p h d -> p (h d)"), start=True, stop=True,
                    skip_group_check=True) for i in range(2)))

                tp.do("pool", f"decay{n}", [f"attn{n}", (f"state{n}", 1)], lambda: nc.gpsimd.tensor_tensor(
                    state[:, b, kp, :, :], state[:, b, kp, :, :],
                    late["bdec"][:, 4 * kp:4 * kp + 4].rearrange("p (i o) -> p i o", o=1).to_broadcast([P, 4, P]),
                    ALU.mult))

                def grow():
                    for i in range(2):
                        h = slice(64 * i, 64 * i + 64)
                        st = state[h, b, kp, :, 64 * i:64 * i + 64]
                        ins = nc.vector.tensor_tensor(st, bk[h, 0:256].rearrange("p (i d) -> p i d", i=4), st, ALU.add)
                    return ins
                tp.do("dve", f"state{n}", [f"grow{n}", f"decay{n}"], grow)
                tp.free(k, f"state{n}")

            def project1(b):
                k, bk, fr = tp.bank()
                tp.do("pe", f"y{b}", [f"o{2 * b + 1}"] + fr, lambda: mms(
                    [(bk[:, 0:P], o_t[:, (2 * b + kp) % 4, i, :], late["wo1"][:, 4 * kp + i, :])
                     for kp in range(2) for i in range(4)]))
                tp.do("dve", f"res3_{b}", [f"y{b}", ("norm2", 1)], lambda: nc.vector.tensor_tensor(
                    res[:, b, :], bk[:, 0:P], x2[:, b, :], ALU.add))
                tp.free(k, f"res3_{b}")

            scores1(0)
            for n in range(8):
                if n < 7:
                    scores1(n + 1)
                attend(n)
                if n in (2, 4, 6):
                    project1(n // 2 - 1)
            for new, old in (("scores_last", "scores71"), ("vdec_last", "vdec7"), ("attn_last", "attn7"),
                             ("grow_last", "grow7"), ("kt_last", "kt1")):
                tp.where[new] = tp.where[old]

            tp.part = "rear"
            project1(3)
            layernorm(tp, 3, "res3_3", res, x3, [("scatter7", 1), ("start", 1)])
            tp.do("act", "x3_again", ["norm3", ("scatter7", 1)], lambda: nc.scalar.copy(x3_rows[:, 1, :, 0:C], x3))

            tp.part = "pre"
            k, bk, fr = tp.bank()
            tp.do("pe", "outproj", ["att_in"] + fr, lambda: last(
                nc.tensor.matmul(bk[:, t * P:(t + 1) * P], att_c[:, t, :], late["wo0"][:, :], start=True, stop=True)
                for t in range(B)))
            tp.do("dve", "res1", ["outproj", "x_in"], lambda: nc.vector.tensor_tensor(
                x_in, bk.rearrange("p (b c) -> p b c", b=B), x_in, ALU.add))
            tp.free(k, "res1")
            layernorm(tp, 1, "res1", x_in, x_in, [])
            if tp.eng is not None and isinstance(it, int) and it == 0:
                prepare(tp.me)

            def choose():
                k, bk, fr = tp.bank()
                tp.do("pe", "gate", ["turned3"] + fr, lambda: last(nc.tensor.matmul(
                    bk[:, 8 * t:8 * t + 8], x3T[:, t, :], late["wgate"][:, :], start=True, stop=True) for t in range(B)))
                tp.do("dve", "logit", ["gate"], lambda: nc.vector.tensor_copy(
                    logit.rearrange("p b e -> p (b e)"), bk[:, 0:32]))
                tp.free(k, "logit")
                tp.do("dve", "top", ["logit"], lambda: last(
                    nc.vector.max(top8[:, t, :], logit[:, t, :]) for t in range(B)), apart=True)
                tp.do("dve", "index", ["top"], lambda: last(
                    nc.vector.max_index(idx8[:, t, :], top8[:, t, :], logit[:, t, :]) for t in range(B)), apart=True)
                tp.do("dve", "gap", ["top"], lambda: nc.vector.tensor_tensor(
                    expd, top8[:, :, 1], top8[:, :, 0], ALU.subtract))
                tp.do("act", "exp", ["gap"], lambda: nc.scalar.activation(wgt[:, 1, :], expd, ACT.Exp))
                tp.do("dve", "indexf", ["index"], lambda: nc.vector.tensor_copy(idxf, idx8))
                tp.do("dve", "onehot", ["indexf", ("count", 1)], lambda: last(nc.vector.tensor_tensor(
                    chosen[:, B * i:B * i + B, :], late["iota"][:, :].rearrange("p (o e) -> p o e", o=1).to_broadcast([P, B, 8]),
                    idxf[:, :, i:i + 1].to_broadcast([P, B, 8]), ALU.is_equal) for i in range(2)))
                tp.do("dve", "denom", ["exp"], lambda: nc.vector.tensor_scalar(
                    wgt[:, 0, :], wgt[:, 1, :], 1.0, None, ALU.add))
                tp.do("dve", "first", ["denom"], lambda: nc.vector.reciprocal(wgt[:, 0, :], wgt[:, 0, :]))
                tp.do("dve", "second", ["first"], lambda: nc.vector.tensor_tensor(
                    wgt[:, 1, :], wgt[:, 1, :], wgt[:, 0, :], ALU.mult))
                tp.do("dve", "picked", ["second", "onehot"], lambda: last(nc.vector.tensor_tensor(
                    pick[:, i, :, :], chosen[:, B * i:B * i + B, :],
                    wgt[:, i, :].rearrange("p (b o) -> p b o", o=1).to_broadcast([P, B, 8]), ALU.mult) for i in range(2)))
                tp.do("dve", "comb", ["picked", ("turn_w", 1)], lambda: nc.vector.tensor_tensor(
                    comb, pick[:, 0, :, :], pick[:, 1, :, :], ALU.add))

            def route():
                k, bk, fr = tp.bank()

                def count():
                    flat = chosen.rearrange("p g e -> p (g e)")
                    n = (TOPK * B + 1) * NE
                    ins = nc.tensor.matmul(bk[:, 0:n], below, flat, start=True, stop=False, skip_group_check=True)
                    for g in range(1, TOPK * B + 1):
                        ins = nc.tensor.matmul(bk[:, NE * g:n], ones, flat[:, 0:n - NE * g], start=False,
                                               stop=(g == TOPK * B), skip_group_check=True)
                    return ins
                tp.do("pe", "count", ["onehot"] + fr, count)
                tp.do("dve", "place", ["count", ("base", 1)], lambda: nc.vector.tensor_tensor(
                    place, bk[:, 0:(TOPK * B + 1) * NE].rearrange("p (g e) -> p g e", e=NE),
                    base.rearrange("p (o e) -> p o e", o=1).to_broadcast([P, TOPK * B + 1, NE]), ALU.add))
                tp.free(k, "place")
                tp.do("dve", "own", ["place"], lambda: nc.vector.tensor_tensor(
                    own, place[:, 0:TOPK * B, :], chosen[:, 0:TOPK * B, :], ALU.mult))
                tp.do("dve", "base", ["place"], lambda: nc.vector.tensor_copy(base, place[:, TOPK * B, :]))
                tp.do("dve", "slotf", ["own"], lambda: nc.vector.tensor_reduce(slotf, own, AX.X, ALU.add))
                tp.do("dve", "slot", ["slotf", ("scatter7", 1)], lambda: nc.vector.tensor_copy(sent, slotf))
                tp.do("dve", "next_token", [("token", 1)], lambda: nc.vector.tensor_scalar(
                    late["token"][:, :], late["token"][:, :], float(P), None, ALU.add))
                tp.do("dve", "token", ["next_token"], lambda: nc.vector.tensor_copy(
                    x3_rows[:, :, :, C].bitcast(U32), late["token"][:, :].rearrange("p (r b) -> p r b", r=TOPK)))
                tp.do("dve", "weight", ["second"], lambda: nc.vector.tensor_copy(x3_rows[:, :, :, C + 1], wgt))

            tp.part = "front"
            hidden(2, hid[1], hid[0], "gelu1_3", {2: lambda: turned(tp, 3, x3, x3T, [("gate", 1), "up_b3"]), 3: choose})
            tp.part = "rear"
            route()
            tp.part = "pre"
            turned(tp, 1, x_in, x1T, ["gate", "up_b3"])
            tp.part = "front"
            k, bk, fr = tp.bank()
            tp.do("pe", "down0", ["gelu2_3"] + fr, lambda: last(mms(
                [(bk[:, t * P:(t + 1) * P], hid[0][:, kk, t * P:(t + 1) * P], late["w3"][:, kk, :])
                 for kk in range(4)]) for t in range(B)))
            tp.do("dve", "res2", ["down0", "norm3"], lambda: nc.vector.tensor_tensor(
                res, bk.rearrange("p (b c) -> p b c", b=B), x1, ALU.add))
            tp.free(k, "res2")
            tp.part = "front"
            layernorm(tp, 2, "res2", res, x2, ["turn2"])
            tp.part = "rear"
            for g in range(TOPK * B):
                tp.do("pool", f"scatter{g}", ["slot", "weight", "x3_again"], lambda: nc.gpsimd.indirect_dma_start(
                    out=rows, out_offset=bass.IndirectOffsetOnAxis(sent[:, g:g + 1], 0),
                    in_=x3_rows[:, g // B, g % B, :], in_offset=None), line="scat", apart=(g == 0))

            tp.part = "rear"
            k, bk, fr = tp.bank()
            tp.do("pe", "turn_w", ["comb"] + fr, lambda: last(nc.tensor.transpose(
                bk[0:8, t * P:(t + 1) * P], comb[:, t, :], ident[:, :]) for t in range(B)))
            tp.do("act", "turned_w", ["turn_w", ("bias", 1), "mul3"], lambda: nc.scalar.copy(combT[0:8, :], bk[0:8, :]))
            tp.free(k, "turned_w")

            k, bk, fr = tp.bank()
            tp.do("pe", "bias", ["turned_w"] + fr, lambda: last(nc.tensor.matmul(
                bk[:, t * P:(t + 1) * P], combT[0:8, t * P:(t + 1) * P], late["b_dn"][0:8, :], start=True, stop=True)
                for t in range(B)))
            tp.do("dve", "start", ["bias", ("stored", 1)], lambda: nc.vector.tensor_tensor(
                acc, bk.rearrange("p (b c) -> p b c", b=B), x3, ALU.add))
            tp.free(k, "start")
            tp.do("act", "stored", ["start"], lambda: nc.scalar.dma_start(
                rest_d[bass.ds(c, 1)].rearrange("c p b k -> p (c b) k"), acc), line="out")
            tp.pad_banks()

        def prepare(me):
            if me == "pool":
                nc.gpsimd.memset(chosen.rearrange("p g e -> p (g e)"), 0.0).then_inc(s_init, 1)
                nc.gpsimd.memset(ones, 1.0).then_inc(s_init, 1)
                nc.gpsimd.memset(state.rearrange("p a b c d -> p (a b c d)"), 0.0).then_inc(s_init, 1)
                for i in range(2):
                    nc.gpsimd.memset(k_one[i].rearrange("p a b -> p (a b)"), 0.0).then_inc(s_init, 1)
            if me == "dve":
                nc.vector.tensor_copy(below, late["before"][:, :]).then_inc(s_init, 1)
                nc.vector.tensor_copy(base, late["region"][:, :]).then_inc(s_init, 1)
            if me == "sp":
                nc.sync.dma_start(w_in, a["w_in"].rearrange("e p m -> p e m")).then_inc(s_experts, 16)
                for g in range(NE):
                    nc.sync.dma_start(rows[NE * REGION + g * P:NE * REGION + (g + 1) * P, :],
                                      a["padding"][(NE + g) * P:(NE + g + 1) * P, :]).then_inc(s_pad, 16)

        def rear(e, me):
            left = {"pe": [(s_pv, NG * NU)], "act": [(s_exp, NS * NU)], "dve": [(s_ta, QC * NU)],
                    "pool": [(s_att[q], 16 * HQ * NU) for q in range(QC)] + [(s_va, NU)], "sp": [(s_late, 16 * len(LATE))]}
            for s, v in left[me]:
                e.wait_ge(s, v)
            e.sem_inc(s_off, 1)
            e.wait_ge(s_off, 5)
            if me == "pool":
                nc.gpsimd.memset(minus_half, -0.5).then_inc(s_init, 1)
                e.wait_ge(s_init, 10)
            if me == "dve":
                nc.vector.tensor_tensor(late["w3"][:, :, :], late["w3"][:, :, :],
                                        late["s3"][:, :].rearrange("p (o c) -> p o c", o=1).to_broadcast([P, 4, C]),
                                        ALU.mult).then_inc(s_cst, 1)
            if me == "pe":
                e.wait_ge(s_cst, CST + 1)
            dry = Tape(None, me, 0, {"pre", "front", "rear"}, None)
            body(dry)

            def run(it, live):
                tp = Tape(e, me, it, live, dry)
                body(tp)
                tp.flush()
            run(0, {"pre"})
            run(1, {"pre", "front"})
            e.wait_ge(s_init, 17)
            with e.Fori(2, NITER - 2) as it:
                run(it, {"pre", "front", "rear"})
            run(NITER - 2, {"front", "rear"})
            if me == "sp":
                e.wait_ge(s_line["pe"], (NITER - 2) * dry.count["pe"] + dry.where["hid2_3"][1])
                e.dma_start(w_dn, a["w_dn"].rearrange("e p m c -> p e (m c)")).then_inc(s_experts, 16)
            run(NITER - 1, {"rear"})
            experts(e, me)

        def experts(e, me):
            if me == "dve":
                tile_table()
            if me in ("sp", "act"):
                e.wait_ge(s_tab, 1)
                for g in range(NE):
                    if g % 2 == (me == "act"):
                        r = e.value_load(table[0:1, 2 * NTILE + g:2 * NTILE + g + 1], min_val=0,
                                         max_val=NE * REGION - P)
                        e.dma_start(rows[bass.ds(r, P), :], a["padding"][g * P:(g + 1) * P, :]).then_inc(s_pad, 16)
            if me in ("sp", "dve"):
                e.wait_ge(s_tab, STEPS_TAB)
            if me == "sp":
                e.wait_ge(s_pad, 16 * 2 * NE)
            left = {"sp": [(s_line["scat"], 16 * TOPK * B * (NITER - 2))], "act": [(s_line["out"], 16 * NITER)]}
            for s, v in left.get(me, []):
                e.wait_ge(s, v)
            e.sem_inc(s_off, 1)
            e.wait_ge(s_off, 10)
            if me in ("pe", "act"):
                e.wait_ge(s_tab, STEPS_TAB)
            if me in ("pe", "dve"):
                e.wait_ge(s_experts, 32)

            def at(j):
                return table[0:1, j:j + 1] if isinstance(j, int) else table[0:1, bass.ds(j, 1)]

            def expert_of(j):
                return e.value_load(at(j), min_val=0, max_val=NE - 1)

            def wait(s, v):
                if not isinstance(v, int) or v > 0:
                    e.wait_ge(s, v)

            def load(J, k):
                r = e.value_load(at(NTILE + XG * J + k), min_val=0, max_val=NE * REGION + NE * P - P)
                wait(s_back[k], 16 * J)
                e.dma_start(x_g[:, k, :], rows[bass.ds(r, P), :]).then_inc(s_xg[k], 16)

            def turn(J, k):
                e.wait_ge(s_xg[k], 16 * (J + 1))
                wait(s_xt, XG * J + k - 1)
                nc.tensor.transpose(banks[:, k % 2, 0:P], x_g[:, k, 0:C], ident[:, :]).then_inc(s_tp, 1)

            def up(J, k):
                e.wait_ge(s_xt, XG * J + k + 1)
                e.wait_ge(s_w1, XG * J + k + 1)
                wait(s_gelu, XG * J + k - 1)
                for m in range(4):
                    ins = nc.tensor.matmul(banks[:, 2 + k % 2, m * P:(m + 1) * P],
                                           w_now[:, k % 4, m * P:(m + 1) * P],
                                           x_gT[:, k % 4, :], start=True, stop=True, skip_group_check=True)
                ins.then_inc(s_up, 1)

            def down(J, k):
                x = expert_of(XG * J + k)
                e.wait_ge(s_gelu, XG * J + k + 1)
                wait(s_y, XG * J + k - 1)
                mms([(banks[:, 4 + k % 2, 0:P], h_g[:, k % 2, m * P:(m + 1) * P],
                      w_dn[:, bass.ds(x, 1), m * P:(m + 1) * P].rearrange("p o m -> p (o m)"))
                     for m in range(4)]).then_inc(s_down, 1)

            def gelu(J, k):
                x = expert_of(XG * J + k)
                e.wait_ge(s_up, XG * J + k + 1)
                wait(s_down, XG * J + k - 1)
                for m in range(4):
                    ins = nc.scalar.activation(h_g[:, k % 2, m * P:(m + 1) * P], banks[:, 2 + k % 2, m * P:(m + 1) * P],
                                               ACT.Gelu, bias=b_in[:, bass.ds(x, 1), m])
                ins.then_inc(s_gelu, 1)

            def take_x(J, k):
                e.wait_ge(s_tp, XG * J + k + 1)
                wait(s_up, XG * J + k - 3)
                nc.vector.tensor_copy(x_gT[:, k % 4, :], banks[:, k % 2, 0:P]).then_inc(s_xt, 1)

            def take_w(J, k):
                x = expert_of(XG * J + k)
                wait(s_up, XG * J + k - 3)
                nc.vector.tensor_copy(w_now[:, k % 4, :], w_in[:, bass.ds(x, 1), :].rearrange("p o m -> p (o m)"))                    .then_inc(s_w1, 1)

            def take_y(J, k):
                e.wait_ge(s_down, XG * J + k + 1)
                wait(s_back[k], 16 * J)
                nc.vector.tensor_scalar(y_g[:, k, :], banks[:, 4 + k % 2, 0:P], x_g[:, k, C + 1:C + 2], None,
                                        ALU.mult).then_inc(s_y, 1)

            def back(J, k):
                e.wait_ge(s_y, XG * J + k + 1)
                e.sem_inc(s_hold, 1)
                nc.gpsimd.indirect_dma_start(
                    out=best, out_offset=bass.IndirectOffsetOnAxis(x_g[:, k, C:C + 1].bitcast(U32), 0),
                    in_=y_g[:, k, :], in_offset=None).then_inc(s_back[k], 16)

            chain = {"sp": [(load, 0)], "pe": [(turn, 3), (up, 1), (down, 0)], "act": [(gelu, 0)],
                     "dve": [(take_x, 3), (take_w, 2), (take_y, 0)], "pool": [(back, 0)]}[me]
            NJ = NTILE // XG
            for fn, ahead in chain:
                for k in range(ahead):
                    fn(0, k)

            def tiles(J, final):
                for k in range(XG):
                    for fn, ahead in chain:
                        if k + ahead < XG:
                            fn(J, k + ahead)
                        elif not final:
                            fn(J + 1, k + ahead - XG)
            tiles(0, False)
            if me == "sp":
                for c in range(T // P):
                    e.dma_start(parts[c][0], rest_d[c]).then_inc(s_rest, 16)
            with e.Fori(1, NJ - 1) as J:
                tiles(J, False)
            tiles(NJ - 1, True)

            NC = T // P
            if me == "sp":
                for k in range(XG):
                    e.wait_ge(s_back[k], 16 * NJ)
            for c in range(NC):
                total, one, two = parts[c]
                if me == "sp":
                    for r, dst in enumerate((one, two)):
                        e.dma_start(dst, best_v[r, c]).then_inc(s_parts[c], 16)
                if me == "pool":
                    e.wait_ge(s_parts[c], 32)
                    nc.gpsimd.tensor_tensor(one, one, two, ALU.add).then_inc(s_both, 1)
                if me == "dve":
                    if c == 0:
                        e.wait_ge(s_rest, 16 * NC)
                    e.wait_ge(s_both, c + 1)
                    nc.vector.tensor_tensor(total, total, one, ALU.add).then_inc(s_d, 1)
                    e.wait_ge(s_d, 3 * c + 1)
                    for t in range(B):
                        ins = nc.vector.bn_stats(st_e[:, c, t, 0:6], total[:, t, :])
                    ins.then_inc(s_d, 1)
                    e.wait_ge(s_d, 3 * c + 2)
                    for t in range(B):
                        ins = nc.vector.bn_aggr(mv_e[:, c, t, :], st_e[:, c, t, 0:6])
                    ins.then_inc(s_d, 1)
                    e.wait_ge(s_d, 3 * c + 3)
                    nc.vector.tensor_scalar(var_e[:, c, :], mv_e[:, c, :, 1], EPS, None, ALU.add).then_inc(s_var4, 1)
                    nc.vector.tensor_scalar(less_e[:, c, :], mv_e[:, c, :, 0], -1.0, None, ALU.mult).then_inc(s_var4, 1)
                def scales(c):
                    e.wait_ge(s_var4, 2 * c + 2)
                    nc.gpsimd.tensor_tensor(rstd_e[:, c, :], var_e[:, c, :], minus_half[:, :], ALU.pow)                        .then_inc(s_rstd4, 1)
                    e.wait_ge(s_rstd4, 2 * c + 1)
                    nc.gpsimd.tensor_tensor(less_e[:, c, :], less_e[:, c, :], rstd_e[:, c, :], ALU.mult)                        .then_inc(s_rstd4, 1)
                if me == "pool":
                    for k in ([c - 1] if c else []) + ([c] if c == NC - 1 else []):
                        scales(k)
                if me == "act":
                    e.wait_ge(s_rstd4, 2 * c + 2)
                    for t in range(B):
                        ins = nc.scalar.activation(one[:, t, :], total[:, t, :], ACT.Identity,
                                                   bias=less_e[:, c, t:t + 1], scale=rstd_e[:, c, t:t + 1])
                    ins.then_inc(s_norm, 1)
                    e.wait_ge(s_norm, c + 1)
                    e.dma_start(out_v[c], one).then_inc(s_out, 16)
            if me == "act":
                e.wait_ge(s_out, 16 * NC)

        def tile_table():
            n = [0]

            def step(ins):
                ins.then_inc(s_tab, 1)
                n[0] += 1
                if n[0] < STEPS_TAB:
                    nc.vector.wait_ge(s_tab, n[0])
            v = nc.vector

            def wide(x, m):
                return x.rearrange("p (o e) -> p o e", o=1).to_broadcast([P, m, x.shape[1]])

            def deep(x, m):
                return x.rearrange("p (e o) -> p e o", o=1).to_broadcast([P, x.shape[1], m])
            step(v.tensor_copy(table[:, 2 * NTILE:2 * NTILE + NE], base))
            step(v.tensor_tensor(t_count, base, late["region"][:, :], ALU.subtract))
            step(v.tensor_tensor(t_cmp, deep(t_count, T * B // P), wide(late["multiples"], NE), ALU.is_gt))
            step(v.tensor_reduce(t_tiles, t_cmp, AX.X, ALU.add))
            step(v.tensor_tensor(t_sq, late["upto"][:, :, :], wide(t_tiles, NE), ALU.mult))
            step(v.tensor_reduce(t_cum, t_sq, AX.X, ALU.add))
            step(v.tensor_tensor(t_ge, wide(t_cum, NTILE), deep(late["number"], NE), ALU.is_le))
            step(v.tensor_reduce(t_expert, t_ge, AX.X, ALU.add))
            step(v.tensor_tensor(t_ge, t_ge, wide(t_tiles, NTILE), ALU.mult))
            step(v.tensor_reduce(t_skip, t_ge, AX.X, ALU.add))
            step(v.tensor_tensor(t_skip, late["number"][:, :], t_skip, ALU.subtract))
            step(v.tensor_scalar(t_skip, t_skip, float(P), None, ALU.mult))
            step(v.scalar_tensor_tensor(out=t_row, in0=t_expert, scalar=float(REGION), in1=t_skip,
                                        op0=ALU.mult, op1=ALU.add))
            step(v.tensor_scalar(t_expert, t_expert, float(NE - 1), None, ALU.min))
            step(v.tensor_copy(table[:, 0:NTILE], t_expert))
            step(v.tensor_copy(table[:, NTILE:2 * NTILE], t_row))
            assert n[0] == STEPS_TAB

        @block.sync
        def _(e):
            for dst, src in ((wqkv[:, :], a["w_qkv"]), (ident[:, :], a["ident"]), (pe_[:, 0, 0:P], a["mask_qk"]),
                             (pe_[:, 1, 0:P], a["mask_kq"])):
                e.dma_start(dst, src).then_inc(s_w, 16)

            for n in range(2 * B):
                e.dma_start(xT[:, n, :], a["xT"][:, n * 512:(n + 1) * 512]).then_inc(s_xT[n], 16)

            def store(b, p):
                e.wait_ge(s_q2, 2 * (2 * b + p) + 2)
                e.wait_ge(s_q3, 2 * (2 * b + p) + 2)
                for w, dst in ((0, q_dst), (1, k_dst)):
                    if w == 0 and b:
                        continue
                    for r in range(PARTS):
                        e.dma_start(dst[b, r, :, :, p * 512:(p + 1) * 512],
                                    qk3[p][w][:, r, :]).then_inc(s_sc[p], 16)

            def stacks(u, p, half):
                cols = slice(512 * half, 512 * half + 512)
                for r in range(PARTS):
                    rows = slice(r * PARTS * D0, (r + 1) * PARTS * D0)
                    e.dma_start(sq[p][rows, :, cols], q_parts[u, :, :, cols].rearrange("h r t -> r h t"))\
                        .then_inc(s_st[p][half], 16)
                    for i in range(PARTS):
                        rows = slice((r * PARTS + i) * D0, (r * PARTS + i + 1) * D0)
                        e.dma_start(sk[p][rows, :, cols], k_parts[u, :, r, :, cols].rearrange("h d t -> d h t"))\
                            .then_inc(s_st[p][half], 16)

            def max_rows(u, p):
                e.wait_ge(s_itc, NI * (u + 1))
                for h in range(HQ):
                    e.dma_start(sq[p][MROW:MROW + PARTS, h, :], mrows[h * PARTS:(h + 1) * PARTS, :])\
                        .then_inc(s_mrow, 16)

            for b in range(B):
                for p in range(2):
                    store(b, p)
                if b == 1:
                    e.wait_ge(s_init, 9)
                    for p in range(2):
                        e.wait_ge(s_sc[p], 16 * 6)
                if b in (1, 2):
                    stacks(0, 0, b - 1)
            for half in range(2):
                stacks(1, 1, half)
            max_rows(0, 0)
            for n in LATE:
                e.dma_start(late[n][:], a[n]).then_inc(s_late, 16)
            for p in range(2):
                e.wait_ge(s_sc[p], 16 * PARTS * (B + 1))
                e.wait_ge(s_sq[p], 16 * PARTS * (B - 1))

            def unit(u, p, first, last, i):
                more = not (isinstance(u, int) and u >= NU - 2)
                if more:
                    e.wait_ge(s_qk, NS * u + FIRST_STEP[HALF_GROUP])
                    stacks(u + 2, p, 0)
                if not last:
                    max_rows(u + 1, 1 - p)
                if more:
                    e.wait_ge(s_qk, NS * (u + 1))
                    stacks(u + 2, p, 1)
            units(e, unit)
            rear(e, 'sp')

        @block.tensor
        def _(e):
            e.wait_ge(s_w, 16 * 4)

            def chunk(b, p, first):
                e.wait_ge(s_xT[2 * b + p], 16)
                if not first:
                    n = 2 * b + p - 1
                    e.wait_ge(s_r1, 2 * n)
                    e.wait_ge(s_v, n)
                for w in range(2):
                    nc.tensor.matmul(banks[:, 4 * p + w, :], wqkv[:, w * C:(w + 1) * C], xT[:, 2 * b + p, :],
                                     start=True, stop=True).then_inc(s_proj, 1)
                for t in range(4):
                    mm_ = nc.tensor.matmul(banks[:, 4 * p + 2, t * P:(t + 1) * P], xT[:, 2 * b + p, t * P:(t + 1) * P],
                                           wqkv[:, 2 * C:3 * C], start=True, stop=True)
                mm_.then_inc(s_proj, 1)
            for p in range(2):
                chunk(0, p, True)
            for b in range(1, B):
                for p in range(2):
                    chunk(b, p, False)
            e.wait_ge(s_r1, 4 * B)
            e.wait_ge(s_v, 2 * B)

            def item(u, p, k, i=None):
                qt, hs, k0, n = ITEMS[k]
                if k == 0:
                    e.wait_ge(s_st[p][0], 16 * 12 * (i + 1))
                if k == HALF_ITEM:
                    e.wait_ge(s_st[p][1], 16 * 12 * (i + 1))
                if not (isinstance(u, int) and u == 0 and k < 2):
                    e.wait_ge(s_itc, NI * u + k - 1)
                for at, h in enumerate(hs):
                    col = at * n if len(hs) == 4 else at * 512
                    dst = pair[k % 2].rearrange("p a c -> p (a c)")[:, col:col + n]
                    diag = k0 + n > qt * P
                    ins = nc.tensor.matmul(dst, sq[p][0:MROW, h, qt * P:(qt + 1) * P], sk[p][0:MROW, h, k0:k0 + n],
                                           start=True, stop=not diag, skip_group_check=True)
                    if diag:
                        ins = nc.tensor.matmul(dst[:, n - P:n], identb[:, :], mask_qk[:, :],
                                               start=False, stop=True, skip_group_check=True)
                ins.then_inc(s_it, 1)

            def turn_max(u):
                k = NI - 1
                e.wait_ge(s_m3, u + 1)
                e.wait_ge(s_itc, NI * u + k - 1)
                dst = pair[k % 2].rearrange("p a c -> p (a c)").bitcast(BF16)
                for qt in range(KT):
                    ins = nc.tensor.transpose(dst[0:HQ * PARTS, qt * P:(qt + 1) * P],
                                              m3[:, qt, :, :].rearrange("p h r -> p (h r)"), identb[:, :])
                ins.then_inc(s_it, 1)

            def scores(u, p, steps):
                for s in steps:
                    if not (isinstance(u, int) and u == 0 and s < NBANK):
                        e.wait_ge(s_exp, NS * u + s - NBANK + 1)
                    bank = score[s % NBANK]
                    for h, kt, q0, n, at in STEPS[s]:
                        ins = nc.tensor.matmul(bank[:, at:at + n], sk[p][0:MROW + PARTS, h, kt * P:(kt + 1) * P],
                                               sq[p][0:MROW + PARTS, h, q0:q0 + n], start=True, stop=True,
                                               skip_group_check=True)
                    ins.then_inc(s_qk, 1)

            def times_v(u, p, g):
                qc, steps = GROUPS[g]
                if g == 0:
                    e.wait_ge(s_va, u + 1)
                if g in (0, 3) and not (isinstance(u, int) and u == 0 and g == 0):
                    e.wait_ge(s_t1, QC * u + qc)
                if g in DIAGONAL:
                    e.wait_ge(s_tri, len(DIAGONAL) * u + DIAGONAL.index(g) + 1)
                else:
                    e.wait_ge(s_exp, NS * u + FIRST_STEP[g] + len(steps))
                pieces = sorted(((h, i, pc) for i, st in enumerate(steps) for pc in [st] for h in {x[0] for x in st}))
                done = []
                for rank in range(2):
                    for h in range(HQ):
                        mine = [(FIRST_STEP[g] + i, x) for i, st in enumerate(steps) for x in st if x[0] == h]
                        if rank < len(mine):
                            s, (_, kt, q0, n, at) = mine[rank]
                            lo = q0 - 512 * qc
                            last = g + 1 == NG or GROUPS[g + 1][0] != qc
                            done.append(nc.tensor.matmul(
                                pv_bank[32 * h:32 * h + 32, lo:lo + n], va[p][:, kt, h, :],
                                pe_[:, s % NSLOT, at:at + n], start=(g in (0, 3)), stop=last,
                                skip_group_check=True))
                done[-1].then_inc(s_pv, 1)

            e.wait_ge(s_cst, CST)
            for k in range(NI - 1):
                item(0, 0, k, 0)
            turn_max(0)

            def unit(u, p, first, last, i):
                for g in range(NG):
                    if g == 0:
                        e.wait_ge(s_mrow, 16 * HQ * (u + 1))
                    steps = range(FIRST_STEP[g], FIRST_STEP[g] + len(GROUPS[g][1]))
                    items = [] if last else list(range(PER_SLOT * g, min(PER_SLOT * g + PER_SLOT, NI - 1)))
                    for n in range(2):
                        scores(u, p, steps[2 * n:2 * n + 2])
                        if items:
                            item(u + 1, 1 - p, items.pop(0), i + p)
                    if g or not first:
                        times_v(*((u, p, g - 1) if g else (u - 1, 1 - p, NG - 1)))
                    for k in items:
                        item(u + 1, 1 - p, k, i + p)
                    if not last and g == CHAIN_SLOT:
                        turn_max(u + 1)
            units(e, unit)
            times_v(NU - 1, 1, NG - 1)
            rear(e, 'pe')

        @block.scalar
        def _(e):
            def chunk(b, p, first):
                n = 2 * b + p
                for w in range(2):
                    e.wait_ge(s_proj, 3 * n + w + 1)
                    if not first:
                        e.wait_ge(s_sc[p], 16 * PARTS * (b + 1))
                        if w == 0 and not (isinstance(b, int) and b == 1):
                            e.wait_ge(s_sq[p], 16 * PARTS * (b - 1))
                    nc.scalar.copy(qk3[p][w][:, 0, :], banks[:, 4 * p + w, :]).then_inc(s_q1, 1)
                for w in range(2):
                    e.wait_ge(s_r1, 2 * n + w + 1)
                    nc.scalar.copy(qk3[p][w][:, 1, :], rest[:, w, :]).then_inc(s_q2, 1)
            for p in range(2):
                chunk(0, p, True)
            for p in range(2):
                chunk(1, p, False)
            with_loop(e, 2, B, lambda b: [chunk(b, p, False) for p in range(2)])

            def unit(u, p, first, last, i):
                for s in range(NS):
                    e.wait_ge(s_qk, NS * u + s + 1)
                    if not (isinstance(u, int) and u == 0 and s < NSLOT):
                        prev = (s - NSLOT) % NS
                        e.wait_ge(s_pv, NG * (u if s >= NSLOT else u - 1) + GROUP_OF[prev] + 1)
                    nc.scalar.activation(pe_[:, s % NSLOT, :], score[s % NBANK], ACT.Exp, scale=SCALE0)\
                        .then_inc(s_exp, 1)
            units(e, unit)
            rear(e, 'act')

        @block.vector
        def _(e):
            e.wait_ge(s_w, 16 * 4)
            for dst, src in ((identb, ident[:, :]), (mask_qk, pe_[:, 0, 0:P]), (mask_kq, pe_[:, 1, 0:P])):
                nc.vector.tensor_copy(dst[:, :], src).then_inc(s_cst, 1)

            def chunk(b, p, first):
                n = 2 * b + p
                for w in range(2):
                    e.wait_ge(s_q1, 2 * n + w + 1)
                    if not (first and p == 0):
                        e.wait_ge(s_q3, 2 * n + w - 1)
                        e.wait_ge(s_q2, 2 * n + w - 1)
                    nc.vector.tensor_tensor(rest[:, w, :], banks[:, 4 * p + w, :], qk3[p][w][:, 0, :], ALU.subtract)\
                        .then_inc(s_r1, 1)
                e.wait_ge(s_proj, 3 * n + 3)
                nc.vector.tensor_copy(
                    vnat[:, bass.ds(4 * b, 4), 4 * p:4 * p + 4, :].rearrange("p j t c -> p t j c"),
                    banks[:, 4 * p + 2, :].rearrange("p (t j c) -> p t j c", t=4, j=4)).then_inc(s_v, 1)
                for w in range(2):
                    e.wait_ge(s_q2, 2 * n + w + 1)
                    nc.vector.tensor_tensor(qk3[p][w][:, 2, :], rest[:, w, :], qk3[p][w][:, 1, :], ALU.subtract)\
                        .then_inc(s_q3, 1)
            for p in range(2):
                chunk(0, p, True)
            with_loop(e, 1, B, lambda b: [chunk(b, p, False) for p in range(2)])
            e.wait_ge(s_init, 9)

            def top(u, k):
                qt, hs, k0, n = ITEMS[k]
                e.wait_ge(s_it, NI * u + k + 1)
                src = pair[k % 2].rearrange("p a c -> p (a c)")
                if len(hs) == 4:
                    src = src[:, 0:4 * n].rearrange("p (h c) -> p h c", c=n)
                else:
                    src = pair[k % 2][:, :, 0:n]
                nc.vector.tensor_reduce(mx[:, 1 if k0 else 0, qt, hs[0]:hs[-1] + 1], src, AX.X, ALU.max)\
                    .then_inc(s_itc, 1)

            def chain(u):
                e.wait_ge(s_itc, NI * u + NI - 1)
                if not (isinstance(u, int) and u == 0):
                    e.wait_ge(s_it, NI * u)
                nc.vector.tensor_tensor(mm, mx[:, 0, :, :], mx[:, 1, :, :], ALU.max).then_inc(s_m, 1)
                e.wait_ge(s_m, 5 * u + 1)
                nc.vector.tensor_scalar(m3[:, :, :, 0], mm, -1.0, None, ALU.mult).then_inc(s_m, 1)
                e.wait_ge(s_m, 5 * u + 2)
                nc.vector.scalar_tensor_tensor(out=mr, in0=mm, scalar=-1.0, in1=m3[:, :, :, 0],
                                               op0=ALU.mult, op1=ALU.subtract).then_inc(s_m, 1)
                e.wait_ge(s_m, 5 * u + 3)
                nc.vector.tensor_copy(m3[:, :, :, 1], mr).then_inc(s_m, 1)
                e.wait_ge(s_m, 5 * u + 4)
                nc.vector.tensor_tensor(m3[:, :, :, 2], mr, m3[:, :, :, 1], ALU.subtract).then_inc(s_m3, 1)
                e.sem_inc(s_m, 1)

            def rows(u):
                k = NI - 1
                e.wait_ge(s_it, NI * u + k + 1)
                if not (isinstance(u, int) and u == 0):
                    e.wait_ge(s_mrow, 16 * HQ * u)
                nc.vector.tensor_copy(mrows[0:HQ * PARTS, :], pair[k % 2].rearrange("p a c -> p (a c)").bitcast(BF16)[0:HQ * PARTS, 0:T])\
                    .then_inc(s_itc, 1)

            def norm(u, qc):
                n = QC * u + qc
                e.wait_ge(s_pv, NG * u + (3 if qc == 0 else NG))
                nc.vector.transpose(tq.rearrange("p a c -> p (a c)"), pv_bank).then_inc(s_t1, 1)
                yield
                e.wait_ge(s_t1, n + 1)
                nc.vector.reciprocal(rl, tq[:, :, D0:D0 + 1]).then_inc(s_n, 1)
                yield
                e.wait_ge(s_n, 2 * n + 1)
                nc.vector.tensor_tensor(tq[:, :, 0:D0], tq[:, :, 0:D0], rl.to_broadcast([P, 16, D0]), ALU.mult)\
                    .then_inc(s_n, 1)
                yield
                e.wait_ge(s_n, 2 * n + 2)
                if not (isinstance(u, int) and u == 0):
                    e.wait_ge(s_att[qc], 16 * HQ * u)
                nc.vector.transpose(ta[:, qc, :], tq.rearrange("p a c -> p (a c)")).then_inc(s_ta, 1)

            for k in range(NI - 1):
                top(0, k)
            chain(0)
            rows(0)

            def unit(u, p, first, last, i):
                pending = iter(())
                for g in range(NG):
                    if g == 0 and not first:
                        pending = norm(u - 1, 1)
                    if g == 3:
                        pending = norm(u, 0)
                    items = [] if last else list(range(PER_SLOT * g, min(PER_SLOT * g + PER_SLOT, NI - 1)))
                    for n, k in enumerate(items):
                        top(u + 1, k)
                        if (g, n) not in ((0, 0), (3, 0), (3, 1)):
                            next(pending, None)
                    if not items:
                        for _ in pending:
                            pass
                    if not last and g == CHAIN_SLOT:
                        chain(u + 1)
                        rows(u + 1)
            units(e, unit)
            for _ in norm(NU - 1, 1):
                pass
            rear(e, 'dve')


        @block.gpsimd
        def _(e):
            for p in range(2):
                nc.gpsimd.memset(sq[p], 0.0).then_inc(s_init, 1)
                nc.gpsimd.memset(sk[p], 0.0).then_inc(s_init, 1)
                nc.gpsimd.memset(va[p], 1.0).then_inc(s_init, 1)
            nc.gpsimd.memset(mx, -3.0e38).then_inc(s_init, 1)
            e.wait_ge(s_init, 7)
            for p in range(2):
                nc.gpsimd.memset(sk[p][MROW:MROW + PARTS, :, :], 1.0).then_inc(s_init, 1)
            e.wait_ge(s_init, 9)

            for n in range(2, 2 * B):
                b, p = divmod(n, 2)
                e.wait_ge(s_q2, 2 * n + 1)
                e.wait_ge(s_q3, 2 * n + 1)
                for r in range(PARTS):
                    e.dma_start(q_dst[b, r, :, :, p * 512:(p + 1) * 512], qk3[p][0][:, r, :]).then_inc(s_sq[p], 16)
            e.wait_ge(s_v, 2 * B)

            def lay_v(u, p):
                if not (isinstance(u, int) and u < 2):
                    e.wait_ge(s_pv, NG * (u - 1))
                nc.gpsimd.tensor_copy(va[p][:, :, :, 0:D0],
                                      vnat[:, bass.ds(u, 1), :, :].rearrange("p u t (h d) -> p (u t) h d", h=HQ))\
                    .then_inc(s_va, 1)
            lay_v(0, 0)
            lay_v(1, 1)

            def triangle(u, g):
                steps = GROUPS[g][1]
                first_slot = FIRST_STEP[g] % NSLOT
                places = sorted({x[4] for x in steps[0] if x[1] * P == x[2]})
                e.wait_ge(s_exp, NS * u + FIRST_STEP[g] + len(steps))
                e.sem_inc(s_hold, 1)
                flat = pe_.rearrange("p s c -> p (s c)")[:, 512 * first_slot:512 * (first_slot + len(steps))]
                blocks = flat.rearrange("p (s c) -> p s c", c=P)
                if places == [0, 256]:
                    views = [blocks[:, 0:4 * len(steps):2, :]]
                else:
                    views = [blocks[:, at // P:4 * len(steps):4, :] for at in places]
                for v in views:
                    ins = nc.gpsimd.affine_select(out=v, in_=v, compare_op=ALU.is_ge, fill=0.0, base=0,
                                                  pattern=[[0, v.shape[1]], [1, P]], channel_multiplier=-1)
                ins.then_inc(s_tri, 1)

            def unit(u, p, first, last, i):
                def store(v, qc):
                    e.wait_ge(s_ta, QC * v + qc + 1)
                    for h in range(HQ):
                        e.dma_start(att_t[v, h, :, qc * 512:(qc + 1) * 512], ta[32 * h:32 * h + D0, qc, :])\
                            .then_inc(s_att[qc], 16)
                for g in range(NG):
                    if g in DIAGONAL:
                        triangle(u, g)
                    if g == 1 and not first:
                        store(u - 1, 1)
                    if g == 5:
                        store(u, 0)
                        if not first and not last:
                            lay_v(u + 1, 1 - p)
                if last:
                    store(u, 1)
            units(e, unit)
            rear(e, 'pool')


def layouts(x):
    a = {}
    f32 = np.float32
    a["xT"] = x["L0_attn_x"].reshape(NT, C).T
    a["x"] = x["L0_attn_x"]
    a["w_qkv"] = x["L0_attn_w_qkv"]
    a["wo0"] = x["L0_attn_w_out"]
    a["w1"], a["w2"] = x["L0_ffn_w1_w"].T, x["L0_ffn_w2_w"].T
    h1, h2, a["w3"] = (x[f"L0_ffn_{n}_w"].T.reshape(4, P, -1).transpose(1, 0, 2) for n in ("h1", "h2", "w3"))
    a["h12"] = np.stack([h1, h2], 1)
    a["s1"], a["s2"], a["sh1"], a["sh2"] = (x[f"L0_ffn_{n}_s"].reshape(4, P).T for n in ("w1", "w2", "h1", "h2"))
    a["s3"] = np.broadcast_to(x["L0_ffn_w3_s"], (P, C))
    order = np.array([[4 * (2 * kp + g) + i for g in range(2)] for kp in range(2) for i in range(4)])
    wq = x["L1_attn_Wq"].reshape(H1, D1, C)
    wk = x["L1_attn_Wk"].reshape(KV1, D1, C)
    a["wq"], a["wk"] = wq[order].reshape(8, P, C).transpose(2, 0, 1), wk.reshape(2, P, C).transpose(2, 0, 1)
    a["wv"] = x["L1_attn_Wv"].T
    a["wo1"] = x["L1_attn_Wo"].T.reshape(H1, D1, C)[order].reshape(8, P, C).transpose(1, 0, 2)
    inv = 1.0 / 10000.0 ** (np.arange(0, D1, 2, dtype=np.float64) / D1)
    ang = np.outer(np.arange(T, dtype=np.float64), inv)
    ang = np.concatenate([ang, ang], axis=1).T
    sign = np.where(np.arange(D1) < D1 // 2, -1.0, 1.0)[:, None]
    a["cos"] = np.tile(np.cos(ang), (2, 1)).astype(f32)
    a["sin"] = np.tile(np.sin(ang) * sign, (2, 1)).astype(f32)
    slope = np.array([2.0 ** (-8.0 / H1 * (i + 1)) for i in range(H1)], f32).astype(np.float64)
    t = np.arange(P, dtype=np.float64)
    gap = t[None, :] - t[:, None]
    a["mask1"] = np.stack([np.where(gap >= 0, np.exp(-sl * np.maximum(gap, 0)), 0.0) for sl in slope], 1)\
        .reshape(P, H1 * P).astype(f32)
    a["qdec"] = np.exp(-slope[order][:, :, None] * (t + 1.0)).repeat(D1, 1).transpose(1, 0, 2).astype(f32)
    a["kdec"] = np.exp(-slope[None, :] * (P - 1.0 - t)[:, None]).astype(f32)
    a["bdec"] = np.exp(-slope[order] * P).repeat(D1, 1).T.astype(f32)
    a["wgate"] = x["L1_ffn_W_gate"]
    a["w_in"] = x["L1_ffn_W_in"]
    a["b_in"] = x["L1_ffn_b_in"].reshape(8, 4, P).transpose(2, 0, 1).reshape(P, 32)
    a["w_dn"] = x["L1_ffn_W_out"].reshape(8, 4, P, C).transpose(0, 2, 1, 3)
    a["b_dn"] = x["L1_ffn_b_out"]
    p = np.arange(P)
    a["before"] = (p[:, None] < p[None, :]).astype(f32)
    group = np.arange(TOPK * B)
    a["token"] = ((group // B) * NT + (group % B) * T - P + p[:, None]).astype(f32)
    a["region"] = np.broadcast_to(REGION * np.arange(NE, dtype=f32), (P, NE))
    a["upto"] = np.broadcast_to(np.tril(np.ones((NE, NE), f32)), (P, NE, NE))
    a["multiples"] = np.broadcast_to(P * np.arange(NT // P, dtype=f32), (P, NT // P))
    a["number"] = np.broadcast_to(np.arange(NTILE, dtype=f32), (P, NTILE))
    padding = np.zeros((2 * NE * P, ROW), np.uint32)
    padding[:, C] = TOPK * NT + np.arange(2 * NE * P)
    a["padding"] = padding.view(f32)
    a["iota"] = np.broadcast_to(np.arange(8, dtype=f32), (P, 8))
    eye = np.eye(P, dtype=np.float32)
    a["ident"] = eye
    upper = np.where(np.arange(P)[:, None] >= np.arange(P)[None, :], 0.0, NEG)
    a["mask_qk"] = upper.astype(f32)
    a["mask_kq"] = upper.T.astype(f32)
    return {k: np.ascontiguousarray(v) for k, v in a.items()}


def kernel(**inputs):
    import concourse.bacc as bacc
    from concourse.bass_utils import run_bass_kernel_spmd

    nc = bacc.Bacc("TRN2", target_bir_lowering=False, num_devices=1)
    arrays = layouts({k: np.asarray(v) for k, v in inputs.items()})
    aps = {k: nc.dram_tensor(f"in_{k}", v.shape, mybir.dt.from_np(v.dtype), kind="ExternalInput").ap()
           for k, v in arrays.items()}
    out = nc.dram_tensor("out_0", (B, T, C), F32, kind="ExternalOutput").ap()
    program(nc, aps, out)
    r = run_bass_kernel_spmd(nc, [{f"in_{k}": v for k, v in arrays.items()}], core_ids=[0])
    return r.results[0]["out_0"]
```
